# Optimizing a Trainium2 kernel written in Bass

```python
import numpy as np
import jax
import jax.numpy as jnp

def _softmax(x, axis=-1):
    return jax.nn.softmax(x, axis=axis)

def _gelu(x):
    return jax.nn.gelu(x, approximate=True)

def _silu(x):
    return jax.nn.silu(x)

def _sigmoid(x):
    return jax.nn.sigmoid(x)

def _layernorm(x, axis=-1, eps=1e-05):
    m = jnp.mean(x, axis=axis, keepdims=True)
    v = jnp.var(x, axis=axis, keepdims=True)
    return (x - m) / jnp.sqrt(v + eps)

def _scatter_add(tgt, idx, src, axis=0):
    return tgt.at[idx].add(src)

def _segment_sum(src, seg, n):
    return jax.ops.segment_sum(src, seg, n)
kernel_name = 'mk_adaln_d1_jaxref_r8_a5ae19'

def setup_inputs(seed: int=0):
    np.random.seed(seed)
    _w = jnp.asarray

    def _L0_attn_setup():
        import jax, jax.numpy as jnp
        import numpy as np
        B, L, D = (4, 128, 128)
        DI, DS, DC, DR = (256, 16, 4, 64)

        def _mamba(x, in_proj, conv_w, conv_b, x_proj, dt_w, dt_b, A_log, Dsk, out_proj):
            xz = x @ in_proj.T
            xh, z = jnp.split(xz, 2, axis=-1)
            xp = jnp.pad(xh, ((0, 0), (DC - 1, 0), (0, 0)))
            Ls = xh.shape[1]
            xc = conv_b + sum((xp[:, k:k + Ls, :] * conv_w[:, k] for k in range(DC)))
            xc = jax.nn.silu(xc)
            dbc = xc @ x_proj.T
            dt, Bm, Cm = jnp.split(dbc, [DR, DR + DS], axis=-1)
            delta = jax.nn.softplus(dt @ dt_w.T + dt_b)
            A = -jnp.exp(A_log)

            def step(h, inp):
                u_t, d_t, B_t, C_t = inp
                h = h * jnp.exp(d_t[:, :, None] * A) + (d_t * u_t)[:, :, None] * B_t[:, None, :]
                return (h, jnp.einsum('bds,bs->bd', h, C_t))
            inps = (jnp.moveaxis(xc, 1, 0), jnp.moveaxis(delta, 1, 0), jnp.moveaxis(Bm, 1, 0), jnp.moveaxis(Cm, 1, 0))
            h0 = jnp.zeros((x.shape[0], DI, DS), x.dtype)
            _, ys = jax.lax.scan(step, h0, inps)
            y = jnp.moveaxis(ys, 0, 1) + xc * Dsk
            y = y * jax.nn.silu(z)
            return y @ out_proj.T
        key = jax.random.key(seed)
        ks = jax.random.split(key, 24)
        rn = lambda k, shape, s=0.02: s * jax.random.normal(k, shape, jnp.float32)
        inp = {'x': jax.random.normal(ks[0], (B, L, D), jnp.float32)}
        for i, p in enumerate(('f', 'b')):
            o = 1 + i * 8
            inp[f'in_proj_{p}'] = rn(ks[o], (2 * DI, D))
            inp[f'conv_w_{p}'] = rn(ks[o + 1], (DI, DC), 0.2)
            inp[f'conv_b_{p}'] = rn(ks[o + 2], (DI,), 0.1)
            inp[f'x_proj_{p}'] = rn(ks[o + 3], (DR + 2 * DS, DI))
            inp[f'dt_w_{p}'] = rn(ks[o + 4], (DI, DR), 0.1)
            inp[f'dt_b_{p}'] = rn(ks[o + 5], (DI,), 0.5)
            inp[f'A_log_{p}'] = jnp.log(jnp.broadcast_to(jnp.arange(1.0, DS + 1.0, dtype=jnp.float32), (DI, DS))) + 0.0
            inp[f'D_{p}'] = jnp.ones((DI,), jnp.float32)
            inp[f'out_proj_{p}'] = rn(ks[o + 6], (D, DI))
        inp['ln_w'] = jnp.ones((D,), jnp.float32)
        inp['ln_b'] = jnp.zeros((D,), jnp.float32)
        return inp
    _L0_attn_in = _L0_attn_setup()

    def _L0_ffn_setup():
        import jax, jax.numpy as jnp
        import numpy as np
        B, S, H, E, K, F = (4, 256, 128, 8, 64, 512)
        key = jax.random.key(seed)
        k0, k1, k2, k3 = jax.random.split(key, 4)
        sc = lambda d: 1.0 / np.sqrt(d).astype(np.float32)
        return {'x': jax.random.normal(k0, (B, S, H), jnp.float32), 'Wg': jax.random.normal(k1, (E, H), jnp.float32) * sc(H), 'W1': jax.random.normal(k2, (E, H, F), jnp.float32) * sc(H), 'b1': jnp.zeros((E, F), jnp.float32), 'W2': jax.random.normal(k3, (E, F, H), jnp.float32) * sc(F), 'b2': jnp.zeros((E, H), jnp.float32)}
    _L0_ffn_in = _L0_ffn_setup()
    _L0_c = _w((lambda *s: np.random.randn(*s).astype(np.float32) * 0.05)(2, 128))
    _L0_wmod = _w((lambda *s: np.random.randn(*s).astype(np.float32) * 0.05)(128, 6 * 128) * 128 ** (-0.5))
    _d = {'L0_attn_x': _L0_attn_in['x'], 'L0_attn_in_proj_f': _L0_attn_in['in_proj_f'], 'L0_attn_conv_w_f': _L0_attn_in['conv_w_f'], 'L0_attn_conv_b_f': _L0_attn_in['conv_b_f'], 'L0_attn_x_proj_f': _L0_attn_in['x_proj_f'], 'L0_attn_dt_w_f': _L0_attn_in['dt_w_f'], 'L0_attn_dt_b_f': _L0_attn_in['dt_b_f'], 'L0_attn_A_log_f': _L0_attn_in['A_log_f'], 'L0_attn_D_f': _L0_attn_in['D_f'], 'L0_attn_out_proj_f': _L0_attn_in['out_proj_f'], 'L0_attn_in_proj_b': _L0_attn_in['in_proj_b'], 'L0_attn_conv_w_b': _L0_attn_in['conv_w_b'], 'L0_attn_conv_b_b': _L0_attn_in['conv_b_b'], 'L0_attn_x_proj_b': _L0_attn_in['x_proj_b'], 'L0_attn_dt_w_b': _L0_attn_in['dt_w_b'], 'L0_attn_dt_b_b': _L0_attn_in['dt_b_b'], 'L0_attn_A_log_b': _L0_attn_in['A_log_b'], 'L0_attn_D_b': _L0_attn_in['D_b'], 'L0_attn_out_proj_b': _L0_attn_in['out_proj_b'], 'L0_attn_ln_w': _L0_attn_in['ln_w'], 'L0_attn_ln_b': _L0_attn_in['ln_b'], 'L0_ffn_Wg': _L0_ffn_in['Wg'], 'L0_ffn_W1': _L0_ffn_in['W1'], 'L0_ffn_b1': _L0_ffn_in['b1'], 'L0_ffn_W2': _L0_ffn_in['W2'], 'L0_ffn_b2': _L0_ffn_in['b2'], 'L0_c': _L0_c, 'L0_wmod': _L0_wmod}
    _x0 = _d['L0_attn_x']
    _d['L0_attn_x'] = jax.random.normal(jax.random.fold_in(jax.random.key(seed), 1), (2, 1024, 128), dtype=_x0.dtype)
    del _x0
    return _d

def reference(L0_attn_x, L0_attn_in_proj_f, L0_attn_conv_w_f, L0_attn_conv_b_f, L0_attn_x_proj_f, L0_attn_dt_w_f, L0_attn_dt_b_f, L0_attn_A_log_f, L0_attn_D_f, L0_attn_out_proj_f, L0_attn_in_proj_b, L0_attn_conv_w_b, L0_attn_conv_b_b, L0_attn_x_proj_b, L0_attn_dt_w_b, L0_attn_dt_b_b, L0_attn_A_log_b, L0_attn_D_b, L0_attn_out_proj_b, L0_attn_ln_w, L0_attn_ln_b, L0_ffn_Wg, L0_ffn_W1, L0_ffn_b1, L0_ffn_W2, L0_ffn_b2, L0_c, L0_wmod):

    def _L0_attn_ref(x, in_proj_f, conv_w_f, conv_b_f, x_proj_f, dt_w_f, dt_b_f, A_log_f, D_f, out_proj_f, in_proj_b, conv_w_b, conv_b_b, x_proj_b, dt_w_b, dt_b_b, A_log_b, D_b, out_proj_b, ln_w, ln_b):
        import jax, jax.numpy as jnp
        import numpy as np
        B, L, D = (4, 128, 128)
        DI, DS, DC, DR = (256, 16, 4, 64)

        def _mamba(x, in_proj, conv_w, conv_b, x_proj, dt_w, dt_b, A_log, Dsk, out_proj):
            xz = x @ in_proj.T
            xh, z = jnp.split(xz, 2, axis=-1)
            xp = jnp.pad(xh, ((0, 0), (DC - 1, 0), (0, 0)))
            Ls = xh.shape[1]
            xc = conv_b + sum((xp[:, k:k + Ls, :] * conv_w[:, k] for k in range(DC)))
            xc = jax.nn.silu(xc)
            dbc = xc @ x_proj.T
            dt, Bm, Cm = jnp.split(dbc, [DR, DR + DS], axis=-1)
            delta = jax.nn.softplus(dt @ dt_w.T + dt_b)
            A = -jnp.exp(A_log)

            def step(h, inp):
                u_t, d_t, B_t, C_t = inp
                h = h * jnp.exp(d_t[:, :, None] * A) + (d_t * u_t)[:, :, None] * B_t[:, None, :]
                return (h, jnp.einsum('bds,bs->bd', h, C_t))
            inps = (jnp.moveaxis(xc, 1, 0), jnp.moveaxis(delta, 1, 0), jnp.moveaxis(Bm, 1, 0), jnp.moveaxis(Cm, 1, 0))
            h0 = jnp.zeros((x.shape[0], DI, DS), x.dtype)
            _, ys = jax.lax.scan(step, h0, inps)
            y = jnp.moveaxis(ys, 0, 1) + xc * Dsk
            y = y * jax.nn.silu(z)
            return y @ out_proj.T
        yf = _mamba(x, in_proj_f, conv_w_f, conv_b_f, x_proj_f, dt_w_f, dt_b_f, A_log_f, D_f, out_proj_f)
        yb = jnp.flip(_mamba(jnp.flip(x, 1), in_proj_b, conv_w_b, conv_b_b, x_proj_b, dt_w_b, dt_b_b, A_log_b, D_b, out_proj_b), 1)
        h = x + yf + yb
        mu = jnp.mean(h, axis=-1, keepdims=True)
        var = jnp.mean(jnp.square(h - mu), axis=-1, keepdims=True)
        return (h - mu) / jnp.sqrt(var + 1e-05) * ln_w + ln_b

    def _L0_ffn_ref(x, Wg, W1, b1, W2, b2):
        import jax, jax.numpy as jnp
        import numpy as np
        B, S, H, E, K, F = (4, 256, 128, 8, 64, 512)
        b, s, h = x.shape
        logits = jnp.einsum('bsh,eh->bse', x, Wg)
        Sm = jnp.swapaxes(jax.nn.softmax(logits, axis=-1), 1, 2)
        G, I = jax.lax.top_k(Sm, K)
        ex = jnp.take_along_axis(x[:, None, :, :], I[..., None], axis=2)
        h1 = jax.nn.gelu(jnp.einsum('bekh,ehf->bekf', ex, W1) + b1[None, :, None, :])
        out = jnp.einsum('bekf,efh->bekh', h1, W2) + b2[None, :, None, :]
        out = G[..., None] * out
        new_x = jnp.zeros_like(x).at[jnp.arange(b)[:, None, None], I].add(out)
        return new_x
    x = L0_attn_x
    mod = (_silu(L0_c) @ L0_wmod).reshape(L0_c.shape[0], 6, 1, -1)
    sa, ca, ga, sb, cb, gb = (mod[:, 0], mod[:, 1], mod[:, 2], mod[:, 3], mod[:, 4], mod[:, 5])
    ga = (2 * (ga >= 0) - 1) * jnp.maximum(jnp.abs(ga), 0.25)
    gb = (2 * (gb >= 0) - 1) * jnp.maximum(jnp.abs(gb), 0.25)
    h = _layernorm(x, axis=-1) * (1 + ca) + sa
    x = x + ga * _L0_attn_ref(h, L0_attn_in_proj_f, L0_attn_conv_w_f, L0_attn_conv_b_f, L0_attn_x_proj_f, L0_attn_dt_w_f, L0_attn_dt_b_f, L0_attn_A_log_f, L0_attn_D_f, L0_attn_out_proj_f, L0_attn_in_proj_b, L0_attn_conv_w_b, L0_attn_conv_b_b, L0_attn_x_proj_b, L0_attn_dt_w_b, L0_attn_dt_b_b, L0_attn_A_log_b, L0_attn_D_b, L0_attn_out_proj_b, L0_attn_ln_w, L0_attn_ln_b)
    h = _layernorm(x, axis=-1) * (1 + cb) + sb
    x = x + gb * _L0_ffn_ref(h, L0_ffn_Wg, L0_ffn_W1, L0_ffn_b1, L0_ffn_W2, L0_ffn_b2)
    return x

_drawn_inputs = setup_inputs


def setup_inputs(seed=0):
    import zlib

    import numpy as np

    out = dict(_drawn_inputs(seed))
    spreads = {'L0_attn_D_f': (1.0, 0.6),
     'L0_attn_D_b': (1.0, 0.6),
     'L0_attn_ln_w': (1.0, 0.2),
     'L0_attn_ln_b': (0.0, 0.3),
     'L0_ffn_b1': (0.0, 0.8),
     'L0_ffn_b2': (0.0, 0.8)}
    factors = {'L0_attn_in_proj_f': 8.0,
     'L0_attn_conv_w_f': 8.0,
     'L0_attn_conv_b_f': 8.0,
     'L0_attn_x_proj_f': 8.0,
     'L0_attn_dt_w_f': 8.0,
     'L0_attn_dt_b_f': 8.0,
     'L0_attn_A_log_f': 8.0,
     'L0_attn_out_proj_f': 8.0,
     'L0_attn_in_proj_b': 8.0,
     'L0_attn_conv_w_b': 8.0,
     'L0_attn_conv_b_b': 8.0,
     'L0_attn_x_proj_b': 8.0,
     'L0_attn_dt_w_b': 8.0,
     'L0_attn_dt_b_b': 8.0,
     'L0_attn_A_log_b': 8.0,
     'L0_attn_out_proj_b': 8.0}
    for name, (base, spread) in spreads.items():
        noise = np.random.default_rng([zlib.crc32(name.encode()), seed]).standard_normal(out[name].shape)
        drawn = base * np.exp(spread * noise) if base else spread * noise
        out[name] = jnp.asarray(drawn.astype(out[name].dtype))
    for name, factor in factors.items():
        out[name] = (out[name] * factor).astype(out[name].dtype)
    return out
```

```python
import numpy as np
import concourse.bass as bass
from concourse import mybir
from contextlib import ExitStack

NB, L, D = 2, 1024, 128
DI, DS, DC, DR = 256, 16, 4, 64
E, TOPK, F = 8, 64, 512
P = 128
NH = DI // P
NBLK = L // P
CH = 512
NCH = L // CH
BPC = CH // P
XD = DR + 2 * DS
NU = 2 * NB
NG = NU * DS
NT = NG * NH
PAD = DC - 1
FC = F // P
NPAIR = E // 2
EPS = 1e-5

WPARTS = [("a_log", 2 * NH * DS), ("dskip", 2 * NH),
          ("in_x", 2 * DI), ("in_z", 2 * DI), ("xproj", 2 * NH * XD), ("outproj", 2 * NH * D),
          ("wg", E), ("b1", E * FC)]
WAT, WCOLS = {}, 0
for _name, _n in WPARTS:
    WAT[_name] = WCOLS
    WCOLS += _n
RPARTS = [("conv_b", 2 * DI), ("dt_b", 2 * DI)]
RAT, RCOLS = {}, 0
for _name, _n in RPARTS:
    RAT[_name] = RCOLS
    RCOLS += _n
CONVW_COLS = 2 * DC * DI

DVE_BLOCKS = 3


SET_VAR, SET_SILUC, SET_NORM, SET_MODT, SET_WEIGHTS, SET_GAB, SET_DONE = range(1, 8)


def prologue_items():
    return ([("X", j) for j in range(4)] + [("Z", j) for j in range(4)] + [("B", j) for j in range(2)]
            + [("BT", 0)] + [("DT", 0), ("DT", 1), ("DU", 0), ("DU", 1), ("DT", 2), ("DT", 3), ("DU", 2), ("DU", 3)])


def epilogue_items():
    return [("YT", j) for j in range(4)] + [("O", j) for j in range(2)]


def item_slots():
    slots = []
    for u in range(NU):
        row = [None] * (2 * DS)
        if u > 0:
            for i, (kind, j) in enumerate(epilogue_items()):
                row[2 + i] = (kind, j, u - 1)
        if u + 1 < NU:
            for i, (kind, j) in enumerate(prologue_items()):
                row[8 + i] = (kind, j, u + 1)
        slots.append(row)
    return slots


SLOTS = item_slots()
ORDER = [(k, j, 0) for k, j in prologue_items()]
ORDER += [it for row in SLOTS for it in row if it is not None]
ORDER += [(k, j, NU - 1) for k, j in epilogue_items()]
NUMBER = {it: n for n, it in enumerate(ORDER)}


def build_block(nc, x_d, mod_d, wpack_d, rows_d, bcast_d, dtw_d, w1_d, w2_d, b2_d, crow_d, out_d):
    fp32 = mybir.dt.float32
    ALU = mybir.AluOpType
    ACT = mybir.ActivationFunctionType
    AX = mybir.AxisListType
    ctx = ExitStack()
    with ctx:
        def sb(name, shape):
            return ctx.enter_context(nc.sbuf_tensor(name, shape, fp32))

        def pb(name, shape):
            return ctx.enter_context(nc.psum_tensor(name, shape, fp32))

        def sem(name):
            return ctx.enter_context(nc.semaphore(name))

        x = sb("x", [P, NB, NBLK, D])
        acc = sb("acc", [P, NB, NBLK, D])
        hT = sb("hT", [P, NB, L + 2 * PAD])
        wp = sb("wp", [P, WCOLS])
        rows = sb("rows", [1, RCOLS])
        lnv = sb("lnv", [P, 2, D])
        dtw = sb("dtw", [DR, 2, DI])
        area1 = sb("area1", [P, 2, 2, NH, L])
        xc = [area1[:, p, 0] for p in range(2)]
        delta = [area1[:, p, 1] for p in range(2)]
        area2 = sb("area2", [P, 2, 2, NBLK, DI])
        duT = [area2[:, p, 0] for p in range(2)]
        gz = [area2[:, p, 1] for p in range(2)]
        bT = sb("bT", [P, 2, NBLK, DS])
        sp_e = sb("sp_e", [P, 2, CH])
        sp_w = sb("sp_w", [P, 2, CH])
        xdbl = sb("xdbl", [XD, L])
        th = sb("th", [P, CH])
        dA = sb("dA", [P, 3, L])
        dBuT = sb("dBuT", [P, 2, NBLK, DI])
        hc = sb("hc", [P, 3, L])
        area3 = sb("area3", [P, 6 + NH, L])
        hs = area3[:, 0:3, :]
        Cb = area3[:, 3:6, :]
        yg = area3[:, 6:6 + NH, :]
        wtap = sb("wtap", [P, 2, DC, DI])
        Aneg = sb("Aneg", [P, 2, NH, DS])
        dskip = sb("dskip", [P, 2, NH, P])
        ident = sb("ident", [P, P])
        ones = sb("ones", [1, P])
        scT = sb("scT", [P, 4, NB])
        modT = sb("modT", [P, 6, NB])
        gmod = sb("gmod", [P, NB, 2, D])
        g1 = sb("g1", [P, NB, D])
        st = sb("st", [P, NB * NBLK, 6])
        mv = sb("mv", [P, NB * NBLK, 2])
        rstd = sb("rstd", [P, NB * NBLK])
        mhalf = sb("mhalf", [P, NB * NBLK])

        yT = pb("yT", [P, NH, NBLK, P])
        dBu = [pb(f"dBu{i}", [P, CH]) for i in range(3)]
        pro = pb("pro", [P, CH])

        s_x = sem("x_loaded")
        s_w = sem("weights_loaded")
        s_c = sem("consts_ready")
        s_set = sem("setup_dve")
        s_seta = sem("setup_act")
        s_setp = sem("setup_pe")
        s_setg = sem("setup_pool")
        pro_ready = sem("pro_ready")
        pro_free = sem("pro_free")
        tanh_ready = sem("tanh_ready")
        ln_ready = sem("ln_ready")
        w_ready = sem("w_ready")
        r_ready = sem("r_ready")
        delta_ready = sem("delta_ready")
        du_ready = sem("du_ready")
        c_stored = sem("c_stored")
        cb_ready = [sem(f"cb_ready{i}") for i in range(3)]
        da_ready = sem("da_ready")
        dbut_act = sem("dbut_act")
        dbut_dve = sem("dbut_dve")
        dbu_ready = sem("dbu_ready")
        scan_done = sem("scan_done")
        hc_done = sem("hc_done")
        yacc_done = sem("yacc_done")
        gate_done = sem("gate_done")
        act_step = sem("act_step")
        dve_step = sem("dve_step")
        var_ready = sem("var_ready")
        rstd_ready = sem("rstd_ready")
        lnx_ready = sem("lnx_ready")
        lnt_ready = sem("lnt_ready")
        h2t_ready = sem("h2t_ready")
        logits_ready = sem("logits_ready")
        shifted = sem("shifted")
        exp_ready = sem("exp_ready")
        sm_ready = sem("sm_ready")
        smt_ready = sem("smt_ready")
        ones_ready = sem("ones_ready")
        pos_ready = sem("pos_ready")
        post_ready = sem("post_ready")
        onehot_ready = sem("onehot_ready")
        gathered = sem("gathered")
        ext_ready = sem("ext_ready")
        gsel_ready = sem("gsel_ready")
        gcol_ready = sem("gcol_ready")
        up_ready = sem("up_ready")
        gelu_ready = sem("gelu_ready")
        turned = sem("onehot_turned")
        kept_act = sem("onehot_kept_act")
        kept_dve = sem("onehot_kept_dve")
        down_ready = sem("down_ready")
        eo_ready = sem("eo_ready")
        scattered = sem("scattered")
        x2_ready = sem("x2_ready")
        s_w1 = sem("w1_loaded")
        s_w2 = sem("w2_loaded")
        s_out = sem("out_stored")

        def w(name, n=None):
            return wp[:, WAT[name]:WAT[name] + (dict(WPARTS)[name] if n is None else n)]

        def unit(u):
            return u // 2, u % 2, u % 2

        def item_done(kind, j, u):
            return NUMBER[(kind, j, u)] + 1

        def chunks(u):
            return range(NCH) if u % 2 == 0 else range(NCH - 1, -1, -1)

        def dt_count(j, u):
            return 4 * u + j + 1

        inx = w("in_x").rearrange("p (d c) -> p d c", d=2)
        wz = w("in_z").rearrange("p (d c) -> p d c", d=2)
        xproj = w("xproj").rearrange("p (d h c) -> p d h c", d=2, h=NH)
        outproj = w("outproj").rearrange("p (d h c) -> p d h c", d=2, h=NH)
        convrow = hc[:, 0:2, :].rearrange("p a b -> p (a b)")
        convw = convrow.rearrange("p (d k c) -> p d k c", d=2, k=DC)
        g0 = area3[:, 2, 0:NB * D].rearrange("p (b d) -> p b d", b=NB)
        gtemp = area3[:, 0:2, :].rearrange("p a b -> p (a b)").rearrange("p (i s) -> p i s", i=4)
        scB = area3[:, 5, 0:NB * P].rearrange("p (b d) -> p b d", b=NB)
        lnw, lnb = lnv[:, 0, :], lnv[:, 1, :]
        modp = area3[:, 4, 0:NB + 6 * D]
        cT, wmod = modp[:, 0:NB], modp[:, NB:NB + 6 * D]
        halfcb = rows[:, RAT["conv_b"]:RAT["conv_b"] + 2 * DI]
        convb = halfcb.rearrange("p (d c) -> p d c", d=2)
        dtb = rows[:, RAT["dt_b"]:RAT["dt_b"] + 2 * DI].rearrange("p (d c) -> p d c", d=2)
        b2r = xdbl[0:1, 0:E * D].rearrange("p (e c) -> p e c", e=E)
        b1c = w("b1").rearrange("p (e c) -> p e c", e=E)

        onehot = area1[:, :, :, :, :].rearrange("p a b c d -> p (a b c d)").rearrange(
            "p (b n s) -> p b n s", b=NB, n=NBLK)
        onehotT = area2[:, :, :, :, :].rearrange("p a b c d -> p (a b c d)").rearrange(
            "p (b q n t) -> p b q n t", b=NB, q=NPAIR, n=NBLK)
        w1s = dBuT[:, :, :, :].rearrange("p a b c -> p (a b c)").rearrange("p (e f) -> p e f", e=E)
        w2s = area3[:, 4:8, :].rearrange("p a b -> p (a b)").rearrange("p (e c h) -> p e c h", e=E, c=FC)
        lnT = hT[:, :, 0:L]
        exT = hc[:, 2, :].rearrange("p (b s) -> p b s", b=NB)
        hid = acc[:, :, :, :].rearrange("p b n d -> p (b n d)").rearrange("p (i s) -> p i s", i=4)
        smT = dA[0:16, 0, :]
        smW = dA[0:16, 1, :]
        pos = dA[0:16, 2, :]
        msk = area3[0:16, 0, :]
        onesr = area3[0:16, 1, :]
        eo = area3[:, 3, :].rearrange("p (b q h) -> p b q h", b=NB, q=NPAIR)
        lnx = hc[:, 0:2, :].rearrange("p b (n d) -> p b n d", n=NBLK)
        lg = th[:, 0:P].rearrange("p (r e) -> p r e", e=E)
        lmax = sb("lmax", [P, NB * NBLK])
        lsum = sb("lsum", [P, NB * NBLK])
        sm = th[:, P:2 * P].rearrange("p (n b e) -> p n b e", n=NBLK, b=NB)
        posT = th[:, 2 * P:3 * P].rearrange("p (n b e) -> p n b e", n=NBLK, b=NB)
        iotak = sb("iotak", [P, TOPK])
        emask = sb("emask", [P, NPAIR, E])
        gcol = sb("gcol", [P, NB, NPAIR])
        gtmp = th[:, 3 * P:3 * P + NB * NPAIR * E].rearrange("p (b q e) -> p b q e", b=NB, q=NPAIR)
        top8 = sb("top8", [16, 8, 8])

        block = ctx.enter_context(nc.Block())

        @block.sync
        def _(sp):
            sp.dma_start(x[:, :, :, :], x_d.rearrange("b (n p) d -> p b n d", p=P)).then_inc(s_x, 16)
            sp.dma_start(modp, mod_d).then_inc(s_w, 16)
            sp.dma_start(wp[:, :], wpack_d).then_inc(s_w, 16)
            sp.dma_start(convrow, bcast_d[0:CONVW_COLS].partition_broadcast(P)).then_inc(s_w, 16)
            sp.dma_start(lnv[:, :, :].rearrange("p a b -> p (a b)"),
                         bcast_d[CONVW_COLS:CONVW_COLS + 2 * D].partition_broadcast(P)).then_inc(s_w, 16)
            sp.dma_start(rows[:, :], rows_d).then_inc(s_w, 16)
            sp.dma_start(dtw[:, :, :], dtw_d).then_inc(s_w, 16)
            for g in range(NG):
                u, s = divmod(g, DS)
                if s == 0:
                    sp.wait_ge(pro_free, item_done("B", 1, u))
                    sp.dma_start(crow_d[u], xdbl[DR + DS:XD, :]).then_inc(c_stored, 16)
                    sp.wait_ge(c_stored, 16 * (u + 1))
                if g >= 3:
                    sp.wait_ge(hc_done, NH * (g - 2))
                sp.dma_start(Cb[:, g % 3, :], crow_d[u, s:s + 1, :].partition_broadcast(P)).then_inc(cb_ready[g % 3], 16)
            sp.wait_ge(dbu_ready, NCH * NT)
            sp.dma_start(w1s, w1_d.rearrange("e h f -> h e f")).then_inc(s_w1, 16)
            sp.wait_ge(hc_done, NT)
            sp.wait_ge(pro_free, len(ORDER))
            sp.dma_start(w2s, w2_d.rearrange("e (c p) h -> p e c h", p=P)).then_inc(s_w2, 16)
            sp.dma_start(b2r, b2_d.rearrange("(o e) d -> o e d", o=1)).then_inc(s_w2, 16)
            for b in range(NB):
                sp.wait_ge(x2_ready, b + 1)
                sp.dma_start(out_d[b].rearrange("(n p) d -> p n d", p=P), x[:, b]).then_inc(s_out, 16)
            sp.wait_ge(s_out, 16 * NB)

        @block.gpsimd
        def _(g_):
            g_.memset(ident[:, :], 0.0).then_inc(s_c, 1)
            g_.memset(ones[:, :], 1.0).then_inc(s_c, 1)
            g_.memset(mhalf[:, :], -0.5).then_inc(s_c, 1)
            g_.memset(hT[:, :, :], 0.0).then_inc(s_c, 1)
            g_.memset(emask[:, :, :], 0.0).then_inc(s_c, 1)
            g_.iota(iotak[:, :], [[1, TOPK]], base=1, channel_multiplier=0,
                    allow_small_or_imprecise_dtypes=True).then_inc(s_c, 1)
            g_.wait_ge(s_c, 6)
            g_.affine_select(out=ident[:, :], in_=ident[:, :], compare_op=ALU.not_equal, fill=1.0, base=0,
                             pattern=[[-1, P]], channel_multiplier=1).then_inc(s_c, 1)
            g_.wait_ge(s_c, 7)
            g_.affine_select(out=emask[0:64, :, :], in_=emask[0:64, :, :], compare_op=ALU.not_equal, fill=1.0,
                             base=0, pattern=[[-2, NPAIR], [1, E]], channel_multiplier=0).then_inc(s_c, 1)
            g_.wait_ge(s_c, 8)
            g_.affine_select(out=emask[64:P, :, :], in_=emask[64:P, :, :], compare_op=ALU.not_equal, fill=1.0,
                             base=-1, pattern=[[-2, NPAIR], [1, E]], channel_multiplier=0).then_inc(s_c, 1)
            g_.wait_ge(s_c, 9)
            g_.wait_ge(s_set, SET_VAR)
            g_.tensor_tensor(rstd[:, :], rstd[:, :], mhalf[:, :], ALU.pow).then_inc(s_setg, 1)

            def pool_r(j, u):
                g_.wait_ge(w_ready, dt_count(j, u))
                g_.tensor_tensor(sp_w[:, j % 2, :], sp_e[:, j % 2, :], sp_w[:, j % 2, :], ALU.subtract).then_inc(r_ready, 1)

            def pool_du(j, u):
                _, _, par = unit(u)
                half, c = divmod(j, NCH)
                g_.wait_ge(delta_ready, dt_count(j, u))
                g_.tensor_tensor(sp_w[:, j % 2, :], delta[par][:, half, c * CH:(c + 1) * CH],
                                 xc[par][:, half, c * CH:(c + 1) * CH], ALU.mult).then_inc(du_ready, 1)

            def items(row, k):
                if row[k] is not None and row[k][0] == "DT":
                    pool_r(row[k][1], row[k][2])
                if k and row[k - 1] is not None and row[k - 1][0] == "DT":
                    pool_du(row[k - 1][1], row[k - 1][2])

            first = [(k, j, 0) for k, j in prologue_items()]
            for k in range(len(first)):
                items(first, k)
            for e in range(NT):
                u, s, half = e // (DS * NH), e // NH % DS, e % NH
                g = e // NH
                g_.wait_ge(scan_done, NCH * (e + 1))
                g_.wait_ge(cb_ready[g % 3], 16 * (g // 3 + 1))
                if e >= 3:
                    g_.wait_ge(yacc_done, e - 2)
                g_.tensor_tensor(hc[:, e % 3, :], hs[:, e % 3, :], Cb[:, g % 3, :], ALU.mult).then_inc(hc_done, 1)
                items(SLOTS[u], NH * s + half)

            g_.wait_ge(hc_done, NT)
            g_.memset(onesr, 1.0).then_inc(ones_ready, 1)
            for n in range(2):
                g_.wait_ge(var_ready, n + 1)
                g_.tensor_tensor(rstd[:, :], rstd[:, :], mhalf[:, :], ALU.pow).then_inc(rstd_ready, 1)

        @block.scalar
        def _(act):
            cnt = [0]

            def then_wait(ins):
                cnt[0] += 1
                ins.then_inc(act_step, 1)
                act.wait_ge(act_step, cnt[0])

            act.wait_ge(s_w, 96)
            nc.scalar.activation(scT[:, 0, :], cT, ACT.Tanh, scale=0.5).then_inc(s_seta, 1)
            nc.scalar.activation(Aneg[:, :, :, :].rearrange("p a b c -> p (a b c)"), w("a_log"), ACT.Exp).then_inc(s_seta, 1)
            act.wait_ge(s_setp, 1)
            act.wait_ge(s_set, SET_MODT)
            act.wait_ge(s_setp, 3)
            act.wait_ge(s_c, 9)
            for b in range(NB):
                nc.scalar.activation(hT[:, b, PAD:PAD + L], yT[:, b].rearrange("p n t -> p (n t)"), ACT.Identity,
                                     bias=modT[:, 0, b:b + 1], scale=modT[:, 1, b:b + 1]).then_inc(s_seta, 1)

            def item_a(kind, j, u):
                b, dr, par = unit(u)
                if kind in ("X", "Z"):
                    act.wait_ge(pro_ready, item_done(kind, j, u))
                    nc.scalar.activation(th[:, :], pro[:, :], ACT.Tanh).then_inc(tanh_ready, 1)
                elif kind == "B":
                    act.wait_ge(pro_ready, item_done(kind, j, u))
                    if u > 0:
                        act.wait_ge(c_stored, 16 * u)
                    nc.scalar.activation(xdbl[:, j * CH:(j + 1) * CH], pro[0:XD, :], ACT.Copy).then_inc(pro_free, 1)
                elif kind == "DT":
                    half, c = divmod(j, NCH)
                    act.wait_ge(pro_ready, item_done(kind, j, u))
                    then_wait(nc.scalar.activation(sp_e[:, j % 2, :], pro[:, :], ACT.Abs))
                    then_wait(nc.scalar.activation(sp_e[:, j % 2, :], sp_e[:, j % 2, :], ACT.Exp, scale=-1.0))
                    nc.scalar.activation(delta[par][:, half, c * CH:(c + 1) * CH], sp_e[:, j % 2, :], ACT.Ln,
                                         bias=1.0).then_inc(ln_ready, 1)
                elif kind == "DU":
                    half, c = divmod(j, NCH)
                    act.wait_ge(pro_ready, item_done(kind, j, u))
                    nc.scalar.activation(duT[par][:, c * BPC:(c + 1) * BPC, half * P:(half + 1) * P],
                                         pro[:, :].rearrange("p (n d) -> p n d", n=BPC), ACT.Copy).then_inc(pro_free, 1)
                elif kind == "YT":
                    half, c = divmod(j, NCH)
                    act.wait_ge(pro_ready, item_done(kind, j, u))
                    nc.scalar.activation(yg[:, half, c * CH:(c + 1) * CH], pro[:, :], ACT.Copy).then_inc(pro_free, 1)

            def exp_tile(e):
                u, s, half = e // (DS * NH), e // NH % DS, e % NH
                _, dr, par = unit(u)
                if s == 0:
                    act.wait_ge(delta_ready, dt_count(NCH * half + NCH - 1, u))
                if e >= 3:
                    act.wait_ge(scan_done, NCH * (e - 2))
                nc.scalar.activation(dA[:, e % 3, :], delta[par][:, half, :], ACT.Exp,
                                     scale=Aneg[:, dr, half, s:s + 1]).then_inc(da_ready, 1)

            na = NBLK - DVE_BLOCKS

            def scale_block(g, n):
                u, s = divmod(g, DS)
                _, _, par = unit(u)
                return nc.scalar.activation(dBuT[:, g % 2, n, :], duT[par][:, n, :], ACT.Copy,
                                            scale=bT[:, par, n, s:s + 1])

            def scale_blocks(g, ns):
                u = g // DS
                if g % DS == 0:
                    act.wait_ge(pro_free, item_done("DU", 3, u))
                if g >= 2:
                    act.wait_ge(dbu_ready, NCH * NH * (g - 1))
                for n in ns:
                    last = scale_block(g, n)
                if n == na - 1:
                    last.then_inc(dbut_act, 1)

            for k, j in prologue_items():
                item_a(k, j, 0)
            exp_tile(0)
            scale_blocks(0, range(na))
            for e in range(NT):
                g, half = divmod(e, NH)
                if e + 1 < NT:
                    exp_tile(e + 1)
                if g + 1 < NG:
                    scale_blocks(g + 1, range(na // 2) if half == 0 else range(na // 2, na))
                it = SLOTS[g // DS][NH * (g % DS) + half]
                if it is not None:
                    item_a(*it)
            for k, j in epilogue_items():
                item_a(k, j, NU - 1)

            for b in range(NB):
                act.wait_ge(lnt_ready, b + 1)
                nc.scalar.activation(lnT[:, b, :], yT[:, b].rearrange("p n t -> p (n t)"), ACT.Identity,
                                     bias=modT[:, 3, b:b + 1], scale=modT[:, 4, b:b + 1]).then_inc(h2t_ready, 1)
            act.wait_ge(shifted, 1)
            nc.scalar.activation(lg[:, :, :], lg[:, :, :], ACT.Exp).then_inc(exp_ready, 1)
            for b in range(NB):
                act.wait_ge(gathered, b + 1)
                nc.scalar.activation(exT[:, b, :], dBu[b][:, :], ACT.Identity,
                                     bias=modT[:, 3, b:b + 1], scale=modT[:, 4, b:b + 1]).then_inc(ext_ready, 1)
            for q in range(NPAIR):
                for e in (2 * q, 2 * q + 1):
                    act.wait_ge(up_ready, e + 1)
                    if e >= 4:
                        act.wait_ge(down_ready, (e - 4) // 2 + 1)
                    for c in range(FC):
                        last = nc.scalar.activation(hid[:, e % 4, c * P:(c + 1) * P], dBu[e % 2][:, c * P:(c + 1) * P],
                                                    ACT.Gelu_apprx_tanh, bias=b1c[:, e, c:c + 1])
                    last.then_inc(gelu_ready, 1)
                act.wait_ge(turned, 2 * q + 1)
                b, qq = divmod(2 * q, NPAIR)
                nc.scalar.activation(onehotT[:, b, qq, :, :], yT[:, 0], ACT.Copy).then_inc(kept_act, 1)

        @block.vector
        def _(dve):
            cnt = [0]

            def step(ins):
                cnt[0] += 1
                ins.then_inc(dve_step, 1)
                dve.wait_ge(dve_step, cnt[0])

            def norm_stats(src):
                for n in range(NB * NBLK):
                    last = nc.vector.bn_stats(st[:, n, :], src(n))
                step(last)
                for n in range(NB * NBLK):
                    last = nc.vector.bn_aggr(mv[:, n, :], st[:, n, :])
                step(last)
                return nc.vector.tensor_scalar(rstd[:, :], mv[:, :, 1], EPS, None, ALU.add)

            dve.wait_ge(s_x, 16)
            norm_stats(lambda n: x[:, n // NBLK, n % NBLK, :]).then_inc(s_set, 1)
            dve.wait_ge(s_w, 96)
            dve.wait_ge(s_seta, 2)
            step(nc.vector.tensor_scalar(scT[:, 1, :], cT, 0.5, None, ALU.mult))
            step(nc.vector.scalar_tensor_tensor(scT[:, 2, :], scT[:, 0, :], 1.0, scT[:, 1, :], ALU.add, ALU.mult))
            for b in range(NB):
                last = nc.vector.tensor_copy(scB[:, b, :], scT[:, 2, b:b + 1].to_broadcast([P, P]))
            last.then_inc(s_set, 1)
            dve.wait_ge(s_setg, 1)
            for n in range(NB * NBLK):
                last = nc.vector.tensor_scalar(acc[:, n // NBLK, n % NBLK, :], x[:, n // NBLK, n % NBLK, :],
                                               mv[:, n, 0:1], rstd[:, n:n + 1], ALU.subtract, ALU.mult)
            last.then_inc(s_set, 1)
            dve.wait_ge(s_setp, 1)
            step(nc.vector.tensor_copy(modT[:, :, :], pro[:, 0:6 * NB].rearrange("p (j b) -> p j b", j=6)))
            nc.vector.tensor_scalar(modT[:, 1, :], modT[:, 1, :], 1.0, None, ALU.add)
            nc.vector.tensor_scalar(modT[:, 4, :], modT[:, 4, :], 1.0, None, ALU.add).then_inc(s_set, 1)
            for dr in range(2):
                for k in range(DC):
                    nc.vector.scalar_tensor_tensor(wtap[:, dr, k, :], convw[:, dr, k, :], 0.5, inx[:, dr, :],
                                                   ALU.mult, ALU.mult)
            nc.vector.tensor_scalar(wz, wz, 0.5, None, ALU.mult)
            nc.vector.tensor_scalar(halfcb, halfcb, 0.5, None, ALU.mult)
            nc.vector.tensor_scalar(Aneg[:, :, :, :], Aneg[:, :, :, :], -1.0, None, ALU.mult)
            dve.wait_ge(s_c, 9)
            for dr in range(2):
                for half in range(NH):
                    at = WAT["dskip"] + dr * NH + half
                    last = nc.vector.tensor_scalar(dskip[:, dr, half, :], ident[:, :], wp[:, at:at + 1], None, ALU.mult)
            last.then_inc(s_set, 1)
            dve.wait_ge(s_setp, 2)
            nc.vector.tensor_copy(gtemp[:, 0, :], dBu[0][:, :]).then_inc(s_set, 1)
            dve.wait_ge(s_set, SET_GAB)
            step(nc.vector.tensor_scalar(gtemp[:, 1, :], gtemp[:, 0, :], 0.0, 2.0, ALU.is_ge, ALU.mult))
            step(nc.vector.scalar_tensor_tensor(gtemp[:, 2, :], gtemp[:, 0, :], -1.0, gtemp[:, 0, :], ALU.mult, ALU.max))
            step(nc.vector.tensor_scalar(gtemp[:, 2, :], gtemp[:, 2, :], 0.25, None, ALU.max))
            step(nc.vector.scalar_tensor_tensor(gmod[:, :, :, :].rearrange("p b g d -> p (b g d)"), gtemp[:, 1, :], -1.0,
                                                gtemp[:, 2, :], ALU.add, ALU.mult))
            for b in range(NB):
                nc.vector.tensor_tensor(g1[:, b, :], gmod[:, b, 0, :], lnw, ALU.mult)
                step(nc.vector.tensor_tensor(g0[:, b, :], gmod[:, b, 0, :], lnb, ALU.mult))
            for b in range(NB):
                last = nc.vector.tensor_tensor(x[:, b], x[:, b], g0[:, b:b + 1, :].to_broadcast([P, NBLK, D]), ALU.add)
            last.then_inc(s_set, 1)

            def item_v(kind, j, u):
                b, dr, par = unit(u)
                if kind == "X":
                    half, c = divmod(j, NCH)
                    dve.wait_ge(tanh_ready, 8 * u + j + 1)
                    nc.vector.scalar_tensor_tensor(xc[par][:, half, c * CH:(c + 1) * CH], th[:, :], 1.0, pro[:, :],
                                                   ALU.add, ALU.mult).then_inc(pro_free, 1)
                elif kind == "Z":
                    dve.wait_ge(tanh_ready, 8 * u + 4 + j + 1)
                    nc.vector.scalar_tensor_tensor(gz[par][:, 2 * j:2 * j + 2, :].rearrange("p n d -> p (n d)"),
                                                   th[:, :], 1.0, pro[:, :], ALU.add, ALU.mult).then_inc(pro_free, 1)
                elif kind == "BT":
                    dve.wait_ge(pro_ready, item_done(kind, j, u))
                    nc.vector.tensor_copy(bT[:, par, :, :],
                                          pro[:, 0:NBLK * 2 * DS].rearrange("p (n s) -> p n s", n=NBLK)[:, :, 0:DS]
                                          ).then_inc(pro_free, 1)
                elif kind == "DT":
                    half, c = divmod(j, NCH)
                    out = delta[par][:, half, c * CH:(c + 1) * CH]
                    dve.wait_ge(ln_ready, dt_count(j, u))
                    nc.vector.tensor_scalar(sp_w[:, j % 2, :], sp_e[:, j % 2, :], 1.0, -1.0, ALU.add, ALU.add).then_inc(w_ready, 1)
                    nc.vector.scalar_tensor_tensor(out, pro[:, :], 0.0, out, ALU.max, ALU.add).then_inc(pro_free, 1)
                elif kind == "O":
                    dst = acc[:, b, j * BPC:(j + 1) * BPC, :].rearrange("p n d -> p (n d)")
                    dve.wait_ge(pro_ready, item_done(kind, j, u))
                    if dr == 0:
                        nc.vector.tensor_copy(dst, pro[:, :]).then_inc(pro_free, 1)
                    else:
                        nc.vector.tensor_tensor(dst, pro[:, :], dst, ALU.add).then_inc(pro_free, 1)

            def finish_delta(j, u):
                _, _, par = unit(u)
                half, c = divmod(j, NCH)
                out = delta[par][:, half, c * CH:(c + 1) * CH]
                dve.wait_ge(pro_free, item_done("DT", j, u))
                dve.wait_ge(r_ready, dt_count(j, u))
                nc.vector.tensor_tensor(out, out, sp_w[:, j % 2, :], ALU.add).then_inc(delta_ready, 1)

            def items(row, k):
                if k and row[k - 1] is not None and row[k - 1][0] == "DT":
                    finish_delta(row[k - 1][1], row[k - 1][2])
                if row[k] is not None:
                    item_v(*row[k])

            def scale_blocks(g):
                u, s = divmod(g, DS)
                _, _, par = unit(u)
                if s == 0:
                    dve.wait_ge(pro_free, item_done("DU", 3, u))
                if g >= 2:
                    dve.wait_ge(dbu_ready, NCH * NH * (g - 1))
                for n in range(NBLK - DVE_BLOCKS, NBLK):
                    last = nc.vector.tensor_scalar(dBuT[:, g % 2, n, :], duT[par][:, n, :],
                                                   bT[:, par, n, s:s + 1], None, ALU.mult)
                last.then_inc(dbut_dve, 1)

            def scan_tile(e):
                u, half = e // (DS * NH), e % NH
                dve.wait_ge(da_ready, e + 1)
                if e >= 3:
                    dve.wait_ge(hc_done, e - 2)
                for i, c in enumerate(chunks(u)):
                    q = NCH * e + i
                    dve.wait_ge(dbu_ready, q + 1)
                    if i:
                        dve.wait_ge(scan_done, q)
                    lo, hi = c * CH, (c + 1) * CH
                    if u % 2 == 0:
                        init = hs[:, e % 3, lo - 1:lo] if i else 0.0
                        nc.vector.tensor_tensor_scan(hs[:, e % 3, lo:hi], dA[:, e % 3, lo:hi], dBu[q % 3][:, :],
                                                     init, ALU.mult, ALU.add).then_inc(scan_done, 1)
                    else:
                        init = hs[:, e % 3, hi:hi + 1] if i else 0.0
                        nc.vector.tensor_tensor_scan(hs[:, e % 3, lo:hi][:, ::-1], dA[:, e % 3, lo:hi][:, ::-1],
                                                     dBu[q % 3][:, ::-1], init, ALU.mult, ALU.add).then_inc(scan_done, 1)

            def gate(u):
                _, _, par = unit(u)
                dve.wait_ge(yacc_done, NH * DS * (u + 1))
                dve.wait_ge(pro_free, item_done("Z", 3, u))
                for half in range(NH):
                    at = gz[par][:, :, half * P:(half + 1) * P]
                    nc.vector.tensor_tensor(at, yT[:, half], at, ALU.mult).then_inc(gate_done, 1)

            first = [(k, j, 0) for k, j in prologue_items()]
            for k in range(len(first)):
                items(first, k)
            scale_blocks(0)
            for e in range(NT):
                g, half = divmod(e, NH)
                u, s = divmod(g, DS)
                scan_tile(e)
                if half == 0 and g + 1 < NG:
                    scale_blocks(g + 1)
                if u > 0 and s == 0 and half == 1:
                    gate(u - 1)
                items(SLOTS[u], NH * s + half)
            gate(NU - 1)
            for k, j in epilogue_items():
                item_v(k, j, NU - 1)

            dve.wait_ge(pro_free, len(ORDER))
            norm_stats(lambda n: acc[:, n // NBLK, n % NBLK, :]).then_inc(var_ready, 1)
            dve.wait_ge(rstd_ready, 1)
            for b in range(NB):
                for n in range(NBLK):
                    r = b * NBLK + n
                    last = nc.vector.tensor_scalar(acc[:, b, n, :], acc[:, b, n, :], mv[:, r, 0:1], rstd[:, r:r + 1],
                                                   ALU.subtract, ALU.mult)
                step(last)
                step(nc.vector.tensor_tensor(acc[:, b], acc[:, b], g1[:, b:b + 1, :].to_broadcast([P, NBLK, D]), ALU.mult))
                step(nc.vector.tensor_tensor(x[:, b], x[:, b], acc[:, b], ALU.add))
            norm_stats(lambda n: x[:, n // NBLK, n % NBLK, :]).then_inc(var_ready, 1)
            dve.wait_ge(rstd_ready, 2)
            for b in range(NB):
                for n in range(NBLK):
                    r = b * NBLK + n
                    last = nc.vector.tensor_scalar(lnx[:, b, n, :], x[:, b, n, :], mv[:, r, 0:1], rstd[:, r:r + 1],
                                                   ALU.subtract, ALU.mult)
                last.then_inc(lnx_ready, 1)
            logits = pro[:, 0:NB * NBLK * E].rearrange("p (r e) -> p r e", e=E)
            dve.wait_ge(logits_ready, 1)
            step(nc.vector.tensor_reduce(lmax[:, :], logits, AX.X, ALU.max))
            nc.vector.tensor_tensor(lg[:, :, :], logits, lmax[:, :].unsqueeze(2).to_broadcast([P, NB * NBLK, E]),
                                    ALU.subtract).then_inc(shifted, 1)
            dve.wait_ge(exp_ready, 1)
            step(nc.vector.tensor_reduce(lsum[:, :], lg[:, :, :], AX.X, ALU.add))
            step(nc.vector.reciprocal(lsum[:, :], lsum[:, :]))
            for b in range(NB):
                rs = slice(b * NBLK, (b + 1) * NBLK)
                last = nc.vector.tensor_tensor(sm[:, :, b, :], lg[:, rs, :],
                                               lsum[:, rs].unsqueeze(2).to_broadcast([P, NBLK, E]), ALU.mult)
            last.then_inc(sm_ready, 1)
            dve.wait_ge(smt_ready, 1)
            for c in range(NCH):
                last = nc.vector.tensor_copy(smT[:, c * CH:(c + 1) * CH], dBu[c][0:16, :])
            step(last)
            for r in range(TOPK // 8):
                src = smT if r == 0 else smW
                step(nc.vector.max(top8[:, r, :], src))
                step(nc.vector.match_replace(smW, top8[:, r, :], src, -1.0))
            step(nc.vector.tensor_scalar(msk, smW, 0.0, None, ALU.is_lt))
            dve.wait_ge(ones_ready, 1)
            step(nc.vector.tensor_tensor_scan(pos, onesr, msk, 0.0, ALU.mult, ALU.add))
            nc.vector.tensor_tensor(pos, pos, msk, ALU.mult).then_inc(pos_ready, 1)
            dve.wait_ge(post_ready, 1)
            step(nc.vector.tensor_copy(posT[:, :, :, :].rearrange("p n b e -> p (n b e)"), pro[:, 0:NB * NBLK * E]))
            for b in range(NB):
                for n in range(NBLK):
                    last = nc.vector.tensor_tensor(onehot[:, b, n, :].rearrange("p (e k) -> p e k", e=E),
                                                   posT[:, n, b, :].unsqueeze(2).to_broadcast([P, E, TOPK]),
                                                   iotak[:, :].unsqueeze(1).to_broadcast([P, E, TOPK]), ALU.is_equal)
                last.then_inc(onehot_ready, 1)
            dve.wait_ge(gsel_ready, 1)
            gsel = pro[:, 0:NB * NPAIR * E].rearrange("p (b q e) -> p b q e", b=NB, q=NPAIR)
            for b in range(NB):
                last = nc.vector.tensor_tensor(gtmp[:, b], gsel[:, b], emask[:, :, :], ALU.mult)
            step(last)
            nc.vector.tensor_reduce(gcol[:, :, :], gtmp[:, :, :, :], AX.X, ALU.add).then_inc(gcol_ready, 1)
            dve.wait_ge(gcol_ready, 1)

            def keep_down(q):
                dve.wait_ge(down_ready, q + 1)
                src = dBu[2] if q % 2 == 0 else pro
                for b in range(NB):
                    last = nc.vector.scalar_tensor_tensor(eo[:, b, q, :], src[:, b * D:(b + 1) * D], gcol[:, b, q:q + 1],
                                                          gmod[:, b, 1, :], ALU.mult, ALU.mult)
                last.then_inc(eo_ready, 1)

            for q in range(NPAIR):
                dve.wait_ge(turned, 2 * q + 2)
                b, qq = divmod(2 * q + 1, NPAIR)
                nc.vector.tensor_copy(onehotT[:, b, qq, :, :], yT[:, 1]).then_inc(kept_dve, 1)
                if q:
                    keep_down(q - 1)
            keep_down(NPAIR - 1)
            for b in range(NB):
                dve.wait_ge(scattered, b + 1)
                nc.vector.tensor_tensor(x[:, b], yT[:, b], x[:, b], ALU.add).then_inc(x2_ready, 1)

        @block.tensor
        def _(pe):
            def mm(out, lhsT, rhs, start, stop):
                return nc.tensor.matmul(out, lhsT, rhs, start=start, stop=stop, skip_group_check=True)

            def turn(out, in_, start, idn=None):
                return nc.tensor.matmul(out, in_, ident[:, :] if idn is None else idn, start=start, stop=True,
                                        is_transpose=True, skip_group_check=True)

            pe.wait_ge(s_w, 96)
            pe.wait_ge(s_c, 9)
            pe.wait_ge(s_set, 2)
            for j in range(6):
                last = mm(pro[:, NB * j:NB * (j + 1)], wmod[:, j * D:(j + 1) * D], scT[:, 2, :], True, True)
            last.then_inc(s_setp, 1)
            for b in range(NB):
                for i, j in enumerate((2, 5)):
                    last = mm(dBu[0][:, (2 * b + i) * D:(2 * b + i + 1) * D], scB[:, b, :],
                              wmod[:, j * D:(j + 1) * D], True, True)
            last.then_inc(s_setp, 1)
            pe.wait_ge(s_set, 3)
            for b in range(NB):
                for n in range(NBLK):
                    last = turn(yT[:, b, n, :], acc[:, b, n, :], True)
            last.then_inc(s_setp, 1)
            pe.wait_ge(s_seta, 4)
            pe.wait_ge(s_set, SET_DONE)

            def item_t(kind, j, u):
                b, dr, par = unit(u)
                n_it = NUMBER[(kind, j, u)]
                if n_it > 0:
                    pe.wait_ge(pro_free, n_it)
                half, c = divmod(j, NCH)
                if kind == "X":
                    for k in range(DC):
                        at = c * CH + (k if dr == 0 else 2 * PAD - k)
                        mm(pro[:, :], wtap[:, dr, k, half * P:(half + 1) * P], hT[:, b, at:at + CH], k == 0, False)
                    last = mm(pro[:, :], convb[:, dr, half * P:(half + 1) * P], ones[:, 0:1].to_broadcast([1, CH]), False, True)
                elif kind == "Z":
                    for i in range(2):
                        at = PAD + (2 * j + i) * P
                        last = mm(pro[:, i * DI:(i + 1) * DI], hT[:, b, at:at + P], wz[:, dr, :], True, True)
                elif kind == "B":
                    for h in range(NH):
                        last = mm(pro[0:XD, :], xproj[:, dr, h, :], xc[par][:, h, j * CH:(j + 1) * CH],
                                  h == 0, h == NH - 1)
                elif kind == "BT":
                    for n in range(NBLK):
                        last = turn(pro[:, n * 2 * DS:(n + 1) * 2 * DS], xdbl[DR:XD, n * P:(n + 1) * P], True,
                                    ident[DR:XD, DR:XD])
                elif kind == "DT":
                    mm(pro[:, :], dtw[:, dr, half * P:(half + 1) * P], xdbl[0:DR, c * CH:(c + 1) * CH], True, False)
                    last = mm(pro[:, :], dtb[:, dr, half * P:(half + 1) * P], ones[:, 0:1].to_broadcast([1, CH]), False, True)
                elif kind == "DU":
                    pe.wait_ge(du_ready, dt_count(j, u))
                    for i in range(BPC):
                        last = turn(pro[:, i * P:(i + 1) * P], sp_w[:, j % 2, i * P:(i + 1) * P], True)
                elif kind == "YT":
                    pe.wait_ge(gate_done, NH * (u + 1))
                    for i in range(BPC):
                        last = turn(pro[:, i * P:(i + 1) * P], gz[par][:, c * BPC + i, half * P:(half + 1) * P], True)
                elif kind == "O":
                    for i in range(BPC):
                        n = j * BPC + i
                        dst = pro[:, i * D:(i + 1) * D]
                        if dr == 0:
                            turn(dst, hT[:, b, PAD + n * P:PAD + (n + 1) * P], True)
                        for h in range(NH):
                            last = mm(dst, yg[:, h, n * P:(n + 1) * P], outproj[:, dr, h, :],
                                      dr == 1 and h == 0, h == NH - 1)
                last.then_inc(pro_ready, 1)

            def dbu_tile(e):
                u, half = e // (DS * NH), e % NH
                g = e // NH
                if half == 0:
                    pe.wait_ge(dbut_act, g + 1)
                    pe.wait_ge(dbut_dve, g + 1)
                for i, c in enumerate(chunks(u)):
                    q = NCH * e + i
                    if q >= 3:
                        pe.wait_ge(scan_done, q - 2)
                    for k in range(BPC):
                        last = turn(dBu[q % 3][:, k * P:(k + 1) * P],
                                    dBuT[:, g % 2, c * BPC + k, half * P:(half + 1) * P], True)
                    last.then_inc(dbu_ready, 1)

            def y_start(u):
                _, dr, par = unit(u)
                if u > 0:
                    pe.wait_ge(gate_done, NH * u)
                for half in range(NH):
                    for n in range(NBLK):
                        mm(yT[:, half, n, :], xc[par][:, half, n * P:(n + 1) * P], dskip[:, dr, half, :],
                           n % BPC == 0, True)

            def y_add(e):
                half = e % NH
                pe.wait_ge(hc_done, e + 1)
                for n in range(NBLK):
                    last = turn(yT[:, half, n, :], hc[:, e % 3, n * P:(n + 1) * P], False)
                last.then_inc(yacc_done, 1)

            for k, j in prologue_items():
                item_t(k, j, 0)
            dbu_tile(0)
            for e in range(NT):
                g, half = divmod(e, NH)
                u, s = divmod(g, DS)
                if e + 1 < NT:
                    dbu_tile(e + 1)
                it = SLOTS[u][NH * s + half]
                if s == 0 and half == 1 and u == 0:
                    y_start(0)
                if e >= 2:
                    y_add(e - 2)
                if s == 0 and half == 1 and u > 0:
                    y_start(u)
                if it is not None:
                    item_t(*it)
            y_add(NT - 2)
            y_add(NT - 1)
            for k, j in epilogue_items():
                item_t(k, j, NU - 1)

            for b in range(NB):
                pe.wait_ge(lnx_ready, b + 1)
                for n in range(NBLK):
                    last = turn(yT[:, b, n, :], lnx[:, b, n, :], True)
                last.then_inc(lnt_ready, 1)
            for b in range(NB):
                pe.wait_ge(h2t_ready, b + 1)
                for n in range(NBLK):
                    r = b * NBLK + n
                    last = mm(pro[:, r * E:(r + 1) * E], lnT[:, b, n * P:(n + 1) * P], w("wg"), True, True)
            last.then_inc(logits_ready, 1)
            pe.wait_ge(sm_ready, 1)
            for n in range(NBLK):
                c, i = divmod(n, BPC)
                last = turn(dBu[c][0:16, i * P:(i + 1) * P], sm[:, n, :, :].rearrange("p b e -> p (b e)"), True)
            last.then_inc(smt_ready, 1)
            pe.wait_ge(pos_ready, 1)
            for n in range(NBLK):
                last = turn(pro[:, n * 16:(n + 1) * 16], pos[:, n * P:(n + 1) * P], True, ident[0:16, 0:16])
            last.then_inc(post_ready, 1)
            for b in range(NB):
                pe.wait_ge(onehot_ready, b + 1)
                for n in range(NBLK):
                    last = mm(dBu[b][:, :], lnx[:, b, n, :], onehot[:, b, n, :], n == 0, n == NBLK - 1)
                last.then_inc(gathered, 1)
            for b in range(NB):
                for q in range(NPAIR):
                    at = (b * NPAIR + q) * E
                    for n in range(NBLK):
                        last = mm(pro[:, at:at + E], onehot[:, b, n, q * P:(q + 1) * P], sm[:, n, b, :],
                                  n == 0, n == NBLK - 1)
            last.then_inc(gsel_ready, 1)
            pe.wait_ge(s_w1, 16)
            pe.wait_ge(s_w2, 32)

            def up(e):
                if e < 2:
                    pe.wait_ge(ext_ready, NB)
                else:
                    pe.wait_ge(gelu_ready, e - 1)
                for c in range(FC):
                    last = mm(dBu[e % 2][:, c * P:(c + 1) * P], w1s[:, e, c * P:(c + 1) * P],
                              exT[:, :, e * TOPK:(e + 1) * TOPK], True, True)
                last.then_inc(up_ready, 1)

            def down(q):
                pe.wait_ge(gelu_ready, 2 * q + 2)
                if q == 1:
                    pe.wait_ge(gcol_ready, 1)
                if q >= 2:
                    pe.wait_ge(eo_ready, q - 1)
                dst = dBu[2] if q % 2 == 0 else pro
                for b in range(NB):
                    for i in range(2):
                        e = 2 * q + i
                        o = dst[i * TOPK:(i + 1) * TOPK, b * D:(b + 1) * D]
                        for c in range(FC):
                            mm(o, hid[:, e % 4, c * P + b * TOPK:c * P + (b + 1) * TOPK], w2s[:, e, c, :], c == 0, False)
                        last = mm(o, ones[:, 0:TOPK], b2r[:, e, :], False, True)
                last.then_inc(down_ready, 1)

            def turn_onehot(m):
                b, q = divmod(m, NPAIR)
                if m >= 2:
                    pe.wait_ge(kept_act if m % 2 == 0 else kept_dve, m // 2)
                for n in range(NBLK):
                    last = turn(yT[:, m % 2, n, :], onehot[:, b, n, q * P:(q + 1) * P], True)
                last.then_inc(turned, 1)

            for q in range(NPAIR):
                up(2 * q)
                up(2 * q + 1)
                turn_onehot(2 * q)
                turn_onehot(2 * q + 1)
                if q:
                    down(q - 1)
            down(NPAIR - 1)
            pe.wait_ge(kept_act, NPAIR)
            pe.wait_ge(kept_dve, NPAIR)
            pe.wait_ge(eo_ready, NPAIR)
            for b in range(NB):
                for n in range(NBLK):
                    for q in range(NPAIR):
                        last = mm(yT[:, b, n, :], onehotT[:, b, q, n, :], eo[:, b, q, :], q == 0, q == NPAIR - 1)
                last.then_inc(scattered, 1)




def kernel(**inputs):
    import concourse.bacc as bacc
    from concourse.bass_utils import run_bass_kernel_spmd

    a = {k: np.asarray(v) for k, v in inputs.items()}

    def both(name, lay):
        return [lay(a[f"L0_attn_{name}_{d}"]) for d in "fb"]

    def halves(m):
        return m.reshape(NH, P, -1).transpose(1, 0, 2).reshape(P, -1)

    wpack = np.concatenate(
        both("A_log", halves) + both("D", halves)
        + both("in_proj", lambda m: m[:DI].T) + both("in_proj", lambda m: m[DI:].T)
        + both("x_proj", lambda m: halves(m.T)) + both("out_proj", lambda m: halves(m.T))
        + [a["L0_ffn_Wg"].T, a["L0_ffn_b1"].reshape(E, FC, P).transpose(2, 0, 1).reshape(P, -1)], axis=1)
    rows = np.concatenate(both("conv_b", lambda m: m) + both("dt_b", lambda m: m))[None]
    bcast = np.concatenate(both("conv_w", lambda m: m.T.reshape(-1)) + [a["L0_attn_ln_w"], a["L0_attn_ln_b"]])
    dtw = np.stack(both("dt_w", lambda m: m.T), axis=1)
    arrays = {"x_in": a["L0_attn_x"], "mod_in": np.concatenate([a["L0_c"].T, a["L0_wmod"]], axis=1), "wpack_in": wpack, "rows_in": rows, "bcast_in": bcast, "dtw_in": dtw,
              "w1_in": a["L0_ffn_W1"], "w2_in": a["L0_ffn_W2"], "b2_in": a["L0_ffn_b2"]}
    arrays = {k: np.ascontiguousarray(v) for k, v in arrays.items()}

    nc = bacc.Bacc("TRN2", target_bir_lowering=False, num_devices=1)
    aps = [nc.dram_tensor(k, v.shape, mybir.dt.from_np(v.dtype), kind="ExternalInput").ap() for k, v in arrays.items()]
    crow = nc.dram_tensor("c_rows", (NU, DS, L), mybir.dt.float32, kind="Internal").ap()
    out = nc.dram_tensor("out", (NB, L, D), mybir.dt.float32, kind="ExternalOutput").ap()
    build_block(nc, *aps, crow, out)
    r = run_bass_kernel_spmd(nc, [arrays], core_ids=[0])
    return r.results[0]["out"]
```

```python
import numpy as np
import concourse.bass as bass
from concourse import mybir
from contextlib import ExitStack

NB, L, D = 2, 1024, 128
DI, DS, DC, DR = 256, 16, 4, 64
E, TOPK, F = 8, 64, 512
P = 128
NH = DI // P
NBLK = L // P
CH = 512
NCH = L // CH
BPC = CH // P
XD = DR + 2 * DS
NU = 2 * NB
NG = NU * DS
NT = NG * NH
PAD = DC - 1
FC = F // P
NPAIR = E // 2
EPS = 1e-5

NBIAS = 2 * 2 * NH

WPARTS = [("a_log", 2 * NH * DS), ("dskip", 2 * NH),
          ("in_x", 2 * DI), ("in_z", 2 * DI), ("xproj", 2 * NH * XD), ("outproj", 2 * NH * D),
          ("wg", E), ("b1", E * FC), ("bias", NBIAS)]
WAT, WCOLS = {}, 0
for _name, _n in WPARTS:
    WAT[_name] = WCOLS
    WCOLS += _n
CONVW_COLS = 2 * DC * DI

OA, OP, SPL = 2, 2, 0
DVE_BLOCKS = 3


SET_VAR, SET_SILUC, SET_NORM, SET_MODT, SET_PARTS, SET_WEIGHTS, SET_BIAS, SET_GAB, SET_DONE = range(1, 10)


FIRST_ITEMS = ([("X", 0), ("X", 2), ("X", 1), ("X", 3), ("B", 0), ("B", 1), ("BT", 0)]
               + [("DT", j) for j in range(4)] + [("DU", j) for j in range(4)])
LAST_ITEMS = [("YT", j) for j in range(4)] + [("O", j) for j in range(2)]


def parts_of(kind):
    return 4 if kind == "X" else 2


def schedule():
    parts = [[] for _ in range(NT)]
    for u in range(NU):
        items = []
        if u + 1 < NU:
            items += [("X", 0, u + 1)]
        else:
            items += [None]
        items += [(k, j, u - 1) for k, j in LAST_ITEMS] if u > 0 else [("Z", j, u) for j in range(4)]
        if u + 1 < NU:
            items += [("X", j, u + 1) for j in range(1, 4)]
            items += [("B", 0, u + 1), ("B", 1, u + 1), ("BT", 0, u + 1)]
            items += [("DT", j, u + 1) for j in range(4)] + [("Z", j, u + 1) for j in range(4)]
            items += [("DU", j, u + 1) for j in range(4)]
        at = NH * DS * u
        for n, it in enumerate(items):
            if it is None:
                at += 2 if n == 0 else 1
                continue
            for p in range(0, parts_of(it[0]), 2):
                parts[at] += [(it, p), (it, p + 1)]
                at += 1
        assert at <= NH * DS * (u + 1) - 2
    ends = [[it for it, p in row if p == parts_of(it[0]) - 1] for row in parts]
    return parts, [row[0] if row else None for row in ends]


PARTS, ENDS = schedule()
LN_AT = 23
ORDER = [(k, j, 0) for k, j in FIRST_ITEMS]
ORDER += [it for it in ENDS if it is not None]
ORDER += [(k, j, NU - 1) for k, j in LAST_ITEMS]
NUMBER = {it: n for n, it in enumerate(ORDER)}
NFIRST = len(FIRST_ITEMS)
BY_ACT = ("B", "DU", "YT")


def count_of(it, kinds):
    return sum(o[0] in kinds for o in ORDER[:NUMBER[it] + 1])


BY_DVE = ("X", "Z", "BT", "DT", "O")


def finish_at(e):
    u, t = divmod(e, DS * NH)
    if u + 1 == NU or t not in (LN_AT + 1, LN_AT + 2):
        return ()
    return (0, 1) if t == LN_AT + 1 else (2, 3)


def build_block(nc, x_d, mod_d, wpack_d, bcast_d, dtw_d, w1_d, w2_d, b2_d, crow_d, out_d):
    fp32 = mybir.dt.float32
    ALU = mybir.AluOpType
    ACT = mybir.ActivationFunctionType
    AX = mybir.AxisListType
    ctx = ExitStack()
    with ctx:
        def sb(name, shape):
            return ctx.enter_context(nc.sbuf_tensor(name, shape, fp32))

        def pb(name, shape):
            return ctx.enter_context(nc.psum_tensor(name, shape, fp32))

        def sem(name):
            return ctx.enter_context(nc.semaphore(name))

        x = sb("x", [P, NB, NBLK, D])
        acc = sb("acc", [P, NB, NBLK, D])
        hT = sb("hT", [P, NB, L + 2 * PAD])
        wp = sb("wp", [P, WCOLS])
        bias3 = ctx.enter_context(nc.sbuf_tensor("bias3", [3, 2, 2, NH, P], mybir.dt.bfloat16))
        ones3 = ctx.enter_context(nc.sbuf_tensor("ones3", [3, 1], mybir.dt.bfloat16))
        part16 = ctx.enter_context(nc.sbuf_tensor("part16", [P, 2, NBIAS], mybir.dt.bfloat16))
        part32 = sb("part32", [P, NBIAS, 3])
        lnv = sb("lnv", [P, 2, D])
        dtw = sb("dtw", [DR, 2, DI])
        area1 = sb("area1", [P, 2, 2, NH, L])
        xc = [area1[:, p, 0] for p in range(2)]
        delta = [area1[:, p, 1] for p in range(2)]
        area2 = sb("area2", [P, 2, 2, NBLK, DI])
        duT = [area2[:, p, 0] for p in range(2)]
        gz = [area2[:, p, 1] for p in range(2)]
        bT = sb("bT", [P, 2, NBLK, DS])
        sp_e = sb("sp_e", [P, NH * NCH, CH])
        xdbl = sb("xdbl", [XD, L])
        th = sb("th", [P, CH])
        dA = sb("dA", [P, 3, L])
        dBuT = sb("dBuT", [P, 2, NBLK, DI])
        hc = sb("hc", [P, 3, L])
        area3 = sb("area3", [P, 6 + NH, L])
        hs = area3[:, 0:3, :]
        Cb = area3[:, 3:6, :]
        yg = area3[:, 6:6 + NH, :]
        sp_w = yg.rearrange("p h (c n) -> p (h c) n", c=NCH)
        wtap = sb("wtap", [P, 2, DC, DI])
        Aneg = sb("Aneg", [P, 2, NH, DS])
        dskip = sb("dskip", [P, 2, NH, P])
        ident = sb("ident", [P, P])
        ones = sb("ones", [1, P])
        scT = sb("scT", [P, 4, NB])
        modT = sb("modT", [P, 6, NB])
        gmod = sb("gmod", [P, NB, 2, D])
        g1 = sb("g1", [P, NB, D])
        st = sb("st", [P, NB * NBLK, 6])
        mv = sb("mv", [P, NB * NBLK, 2])
        rstd = sb("rstd", [P, NB * NBLK])
        mhalf = sb("mhalf", [P, NB * NBLK])

        yT = pb("yT", [P, NH, NBLK, P])
        dBu = [pb(f"dBu{i}", [P, CH]) for i in range(3)]
        pro = pb("pro", [P, CH])

        def bank(it):
            n = NUMBER[it]
            return [pro, yT[:, 0, 0:BPC], yT[:, 0, BPC:NBLK], yT[:, 1, 0:BPC], yT[:, 1, BPC:NBLK]][n % 5] if n < NFIRST else pro

        def flat(b):
            return b[:, :] if len(b.shape) == 2 else b.rearrange("p n t -> p (n t)")

        def th_of(it):
            return th[:, :] if NUMBER[it] >= NFIRST else hs[:, 0, (NUMBER[it] % 2) * CH:(NUMBER[it] % 2 + 1) * CH]

        s_x = sem("x_loaded")
        s_w = sem("weights_loaded")
        s_c = sem("consts_ready")
        s_set = sem("setup_dve")
        s_seta = sem("setup_act")
        s_setp = sem("setup_pe")
        s_setg = sem("setup_pool")
        pro_ready = sem("pro_ready")
        item_act = sem("item_act")
        item_dve = sem("item_dve")
        tanh_ready = sem("tanh_ready")
        ln_ready = sem("ln_ready")
        e_ready = sem("e_ready")
        w_ready = sem("w_ready")
        r_ready = sem("r_ready")
        delta_ready = sem("delta_ready")
        du_ready = sem("du_ready")
        c_stored = sem("c_stored")
        cb_ready = [sem(f"cb_ready{i}") for i in range(3)]
        da_ready = sem("da_ready")
        dbut_act = sem("dbut_act")
        dbut_dve = sem("dbut_dve")
        dbu_ready = sem("dbu_ready")
        scan_done = sem("scan_done")
        hc_done = sem("hc_done")
        yacc_done = sem("yacc_done")
        gate_done = sem("gate_done")
        act_step = sem("act_step")
        dve_step = sem("dve_step")
        var_ready = sem("var_ready")
        rstd_ready = sem("rstd_ready")
        lnx_ready = sem("lnx_ready")
        lnt_ready = sem("lnt_ready")
        h2t_ready = sem("h2t_ready")
        logits_ready = sem("logits_ready")
        shifted = sem("shifted")
        exp_ready = sem("exp_ready")
        sm_ready = sem("sm_ready")
        smt_ready = sem("smt_ready")
        ones_ready = sem("ones_ready")
        pos_ready = sem("pos_ready")
        post_ready = sem("post_ready")
        onehot_ready = sem("onehot_ready")
        gathered = sem("gathered")
        ext_ready = sem("ext_ready")
        gsel_ready = sem("gsel_ready")
        gcol_ready = sem("gcol_ready")
        up_ready = sem("up_ready")
        gelu_ready = sem("gelu_ready")
        turned = sem("onehot_turned")
        kept_act = sem("onehot_kept_act")
        kept_dve = sem("onehot_kept_dve")
        down_ready = sem("down_ready")
        eo_ready = sem("eo_ready")
        scattered = sem("scattered")
        x2_ready = sem("x2_ready")
        s_w1 = sem("w1_loaded")
        s_w2 = sem("w2_loaded")
        s_out = sem("out_stored")

        def w(name, n=None):
            return wp[:, WAT[name]:WAT[name] + (dict(WPARTS)[name] if n is None else n)]

        def unit(u):
            return u // 2, u % 2, u % 2

        def wait_item(eng, *it):
            if it[0] in BY_ACT:
                eng.wait_ge(item_act, count_of(it, BY_ACT))
            else:
                eng.wait_ge(item_dve, count_of(it, BY_DVE))

        def chunks(u):
            return range(NCH) if u % 2 == 0 else range(NCH - 1, -1, -1)

        def dt_count(j, u):
            return 4 * u + j + 1

        inx = w("in_x").rearrange("p (d c) -> p d c", d=2)
        wz = w("in_z").rearrange("p (d c) -> p d c", d=2)
        xproj = w("xproj").rearrange("p (d h c) -> p d h c", d=2, h=NH)
        outproj = w("outproj").rearrange("p (d h c) -> p d h c", d=2, h=NH)
        convrow = hc[:, 0:2, :].rearrange("p a b -> p (a b)")
        convw = convrow.rearrange("p (d k c) -> p d k c", d=2, k=DC)
        g0 = area3[:, 2, 0:NB * D].rearrange("p (b d) -> p b d", b=NB)
        gtemp = area3[:, 0:2, :].rearrange("p a b -> p (a b)").rearrange("p (i s) -> p i s", i=4)
        scB = area3[:, 5, 0:NB * P].rearrange("p (b d) -> p b d", b=NB)
        lnw, lnb = lnv[:, 0, :], lnv[:, 1, :]
        modp = area3[:, 4, 0:NB + 6 * D]
        cT, wmod = modp[:, 0:NB], modp[:, NB:NB + 6 * D]
        biasc = w("bias")
        b2r = xdbl[0:1, 0:E * D].rearrange("p (e c) -> p e c", e=E)
        b1c = w("b1").rearrange("p (e c) -> p e c", e=E)

        onehot = area1[:, :, :, :, :].rearrange("p a b c d -> p (a b c d)").rearrange(
            "p (b n s) -> p b n s", b=NB, n=NBLK)
        onehotT = area2[:, :, :, :, :].rearrange("p a b c d -> p (a b c d)").rearrange(
            "p (b q n t) -> p b q n t", b=NB, q=NPAIR, n=NBLK)
        w1s = dBuT[:, :, :, :].rearrange("p a b c -> p (a b c)").rearrange("p (e f) -> p e f", e=E)
        w2s = area3[:, 4:8, :].rearrange("p a b -> p (a b)").rearrange("p (e c h) -> p e c h", e=E, c=FC)
        lnT = hT[:, :, 0:L]
        exT = hc[:, 2, :].rearrange("p (b s) -> p b s", b=NB)
        hid = acc[:, :, :, :].rearrange("p b n d -> p (b n d)").rearrange("p (i s) -> p i s", i=4)
        smT = dA[0:16, 0, :]
        smW = dA[0:16, 1, :]
        pos = dA[0:16, 2, :]
        msk = area3[0:16, 0, :]
        onesr = area3[0:16, 1, :]
        eo = area3[:, 3, :].rearrange("p (b q h) -> p b q h", b=NB, q=NPAIR)
        lnx = hc[:, 0:2, :].rearrange("p b (n d) -> p b n d", n=NBLK)
        lg = th[:, 0:P].rearrange("p (r e) -> p r e", e=E)
        lmax = sb("lmax", [P, NB * NBLK])
        lsum = sb("lsum", [P, NB * NBLK])
        sm = th[:, P:2 * P].rearrange("p (n b e) -> p n b e", n=NBLK, b=NB)
        posT = th[:, 2 * P:3 * P].rearrange("p (n b e) -> p n b e", n=NBLK, b=NB)
        iotak = sb("iotak", [P, TOPK])
        emask = sb("emask", [P, NPAIR, E])
        gcol = sb("gcol", [P, NB, NPAIR])
        gtmp = th[:, 3 * P:3 * P + NB * NPAIR * E].rearrange("p (b q e) -> p b q e", b=NB, q=NPAIR)
        top8 = sb("top8", [16, 8, 8])

        block = ctx.enter_context(nc.Block())

        @block.sync
        def _(sp):
            sp.dma_start(x[:, :, :, :], x_d.rearrange("b (n p) d -> p b n d", p=P)).then_inc(s_x, 16)
            sp.dma_start(modp, mod_d).then_inc(s_w, 16)
            sp.dma_start(wp[:, :], wpack_d).then_inc(s_w, 16)
            sp.dma_start(convrow, bcast_d[0:CONVW_COLS].partition_broadcast(P)).then_inc(s_w, 16)
            sp.dma_start(lnv[:, :, :].rearrange("p a b -> p (a b)"),
                         bcast_d[CONVW_COLS:CONVW_COLS + 2 * D].partition_broadcast(P)).then_inc(s_w, 16)
            sp.dma_start(dtw[:, :, :], dtw_d).then_inc(s_w, 16)
            for g in range(NG):
                u, s = divmod(g, DS)
                if s == 0:
                    wait_item(sp, "B", 1, u)
                    sp.dma_start(crow_d[u], xdbl[DR + DS:XD, :]).then_inc(c_stored, 16)
                    sp.wait_ge(c_stored, 16 * (u + 1))
                if g >= 3:
                    sp.wait_ge(hc_done, NH * (g - 2))
                sp.dma_start(Cb[:, g % 3, :], crow_d[u, s:s + 1, :].partition_broadcast(P)).then_inc(cb_ready[g % 3], 16)
            sp.wait_ge(dbu_ready, NCH * NT)
            sp.dma_start(w1s, w1_d.rearrange("e h f -> h e f")).then_inc(s_w1, 16)
            sp.wait_ge(hc_done, NT)
            wait_item(sp, "O", 1, NU - 1)
            sp.dma_start(w2s, w2_d.rearrange("e (c p) h -> p e c h", p=P)).then_inc(s_w2, 16)
            sp.dma_start(b2r, b2_d.rearrange("(o e) d -> o e d", o=1)).then_inc(s_w2, 16)
            for b in range(NB):
                sp.wait_ge(x2_ready, b + 1)
                sp.dma_start(out_d[b].rearrange("(n p) d -> p n d", p=P), x[:, b]).then_inc(s_out, 16)
            sp.wait_ge(s_out, 16 * NB)

        @block.gpsimd
        def _(g_):
            g_.memset(ident[:, :], 0.0).then_inc(s_c, 1)
            g_.memset(ones[:, :], 1.0).then_inc(s_c, 1)
            g_.memset(mhalf[:, :], -0.5).then_inc(s_c, 1)
            g_.memset(ones3[:, :], 1.0).then_inc(s_c, 1)
            g_.memset(hT[:, :, :], 0.0).then_inc(s_c, 1)
            g_.memset(emask[:, :, :], 0.0).then_inc(s_c, 1)
            g_.iota(iotak[:, :], [[1, TOPK]], base=1, channel_multiplier=0,
                    allow_small_or_imprecise_dtypes=True).then_inc(s_c, 1)
            g_.wait_ge(s_c, 7)
            g_.affine_select(out=ident[:, :], in_=ident[:, :], compare_op=ALU.not_equal, fill=1.0, base=0,
                             pattern=[[-1, P]], channel_multiplier=1).then_inc(s_c, 1)
            g_.wait_ge(s_c, 8)
            g_.affine_select(out=emask[0:64, :, :], in_=emask[0:64, :, :], compare_op=ALU.not_equal, fill=1.0,
                             base=0, pattern=[[-2, NPAIR], [1, E]], channel_multiplier=0).then_inc(s_c, 1)
            g_.wait_ge(s_c, 9)
            g_.affine_select(out=emask[64:P, :, :], in_=emask[64:P, :, :], compare_op=ALU.not_equal, fill=1.0,
                             base=-1, pattern=[[-2, NPAIR], [1, E]], channel_multiplier=0).then_inc(s_c, 1)
            g_.wait_ge(s_c, 10)
            g_.wait_ge(s_set, SET_VAR)
            g_.tensor_tensor(rstd[:, :], rstd[:, :], mhalf[:, :], ALU.pow).then_inc(s_setg, 1)

            def pool_r(j, u):
                g_.wait_ge(w_ready, dt_count(j, u))
                g_.tensor_tensor(sp_w[:, j, :], sp_e[:, j, :], sp_w[:, j, :], ALU.subtract).then_inc(r_ready, 1)

            def pool_du(j, u):
                _, _, par = unit(u)
                half, c = divmod(j, NCH)
                g_.wait_ge(delta_ready, dt_count(j, u))
                g_.tensor_tensor(sp_w[:, j, :], delta[par][:, half, c * CH:(c + 1) * CH],
                                 xc[par][:, half, c * CH:(c + 1) * CH], ALU.mult).then_inc(du_ready, 1)

            for j in range(4):
                pool_r(j, 0)
            for j in range(4):
                pool_du(j, 0)
            for e in range(NT):
                g = e // NH
                for j in finish_at(e):
                    pool_du(j, e // (DS * NH) + 1)
                g_.wait_ge(scan_done, NCH * (e + 1))
                g_.wait_ge(cb_ready[g % 3], 16 * (g // 3 + 1))
                if e >= 3:
                    g_.wait_ge(yacc_done, e - 2)
                g_.tensor_tensor(hc[:, e % 3, :], hs[:, e % 3, :], Cb[:, g % 3, :], ALU.mult).then_inc(hc_done, 1)
                if e >= 1 and ENDS[e - 1] is not None and ENDS[e - 1][0] == "DT":
                    pool_r(*ENDS[e - 1][1:])

            g_.wait_ge(hc_done, NT)
            g_.memset(onesr, 1.0).then_inc(ones_ready, 1)
            for n in range(2):
                g_.wait_ge(var_ready, n + 1)
                g_.tensor_tensor(rstd[:, :], rstd[:, :], mhalf[:, :], ALU.pow).then_inc(rstd_ready, 1)

        @block.scalar
        def _(act):
            cnt = [0]

            def then_wait(ins):
                cnt[0] += 1
                ins.then_inc(act_step, 1)
                act.wait_ge(act_step, cnt[0])

            act.wait_ge(s_w, 80)
            nc.scalar.activation(scT[:, 0, :], cT, ACT.Tanh, scale=0.5).then_inc(s_seta, 1)
            nc.scalar.activation(Aneg[:, :, :, :].rearrange("p a b c -> p (a b c)"), w("a_log"), ACT.Exp).then_inc(s_seta, 1)
            act.wait_ge(s_setp, 1)
            act.wait_ge(s_set, SET_MODT)
            act.wait_ge(s_setp, 3)
            act.wait_ge(s_c, 10)
            for b in range(NB):
                nc.scalar.activation(hT[:, b, PAD:PAD + L], yT[:, b].rearrange("p n t -> p (n t)"), ACT.Identity,
                                     bias=modT[:, 0, b:b + 1], scale=modT[:, 1, b:b + 1]).then_inc(s_seta, 1)

            def item_a(kind, j, u):
                b, dr, par = unit(u)
                it = (kind, j, u)
                src = flat(bank(it))
                half, c = divmod(j, NCH)
                if kind not in ("BT", "O"):
                    act.wait_ge(pro_ready, NUMBER[it] + 1)
                if kind in ("X", "Z"):
                    if it in ORDER[2:NFIRST]:
                        wait_item(act, *ORDER[NUMBER[it] - 2])
                    nc.scalar.activation(th_of(it), src, ACT.Tanh).then_inc(tanh_ready, 1)
                elif kind == "B":
                    if u > 0:
                        act.wait_ge(c_stored, 16 * u)
                    nc.scalar.activation(xdbl[:, j * CH:(j + 1) * CH], src[0:XD, :], ACT.Copy).then_inc(item_act, 1)
                elif kind == "DT":
                    then_wait(nc.scalar.activation(sp_e[:, j, :], src, ACT.Abs))
                    nc.scalar.activation(sp_e[:, j, :], sp_e[:, j, :], ACT.Exp, scale=-1.0).then_inc(e_ready, 1)
                elif kind == "DU":
                    nc.scalar.activation(duT[par][:, c * BPC:(c + 1) * BPC, half * P:(half + 1) * P],
                                         src.rearrange("p (n d) -> p n d", n=BPC), ACT.Copy).then_inc(item_act, 1)
                elif kind == "YT":
                    nc.scalar.activation(yg[:, half, c * CH:(c + 1) * CH], src, ACT.Copy).then_inc(item_act, 1)

            def logs(u):
                for j in range(NH * NCH):
                    act.wait_ge(r_ready, dt_count(j, u))
                    nc.scalar.activation(sp_e[:, j, :], sp_e[:, j, :], ACT.Ln, bias=1.0).then_inc(ln_ready, 1)

            def exp_tile(e):
                u, s, half = e // (DS * NH), e // NH % DS, e % NH
                _, dr, par = unit(u)
                if s == 0:
                    act.wait_ge(delta_ready, dt_count(NCH * half + NCH - 1, u))
                if e >= 3:
                    act.wait_ge(scan_done, NCH * (e - 2))
                nc.scalar.activation(dA[:, e % 3, :], delta[par][:, half, :], ACT.Exp,
                                     scale=Aneg[:, dr, half, s:s + 1]).then_inc(da_ready, 1)

            na = NBLK - DVE_BLOCKS

            def scale_block(g, n):
                u, s = divmod(g, DS)
                _, _, par = unit(u)
                return nc.scalar.activation(dBuT[:, g % 2, n, :], duT[par][:, n, :], ACT.Copy,
                                            scale=bT[:, par, n, s:s + 1])

            def scale_blocks(g, ns):
                u = g // DS
                if g % DS == 0:
                    wait_item(act, "DU", 3, u)
                    wait_item(act, "BT", 0, u)
                if g >= 2:
                    act.wait_ge(dbu_ready, NCH * NH * (g - 1))
                for n in ns:
                    last = scale_block(g, n)
                if n == na - 1:
                    last.then_inc(dbut_act, 1)

            for k, j in FIRST_ITEMS:
                if k == "DU" and j == 0:
                    logs(0)
                item_a(k, j, 0)
            exp_tile(0)
            scale_blocks(0, range(na))
            for e in range(NT):
                g, half = divmod(e, NH)
                def it():
                    if e and ENDS[e - 1] is not None:
                        item_a(*ENDS[e - 1])
                if OA == 0: it()
                if e + 1 < NT:
                    exp_tile(e + 1)
                if OA == 1: it()
                if g + 1 < NG:
                    scale_blocks(g + 1, range(na // 2+ SPL) if half == 0 else range(na // 2+SPL, na))
                if OA == 2: it()
                if e % (DS * NH) == LN_AT and g // DS + 1 < NU:
                    logs(g // DS + 1)
            for k, j in LAST_ITEMS:
                item_a(k, j, NU - 1)

            for b in range(NB):
                act.wait_ge(lnt_ready, b + 1)
                nc.scalar.activation(lnT[:, b, :], yT[:, b].rearrange("p n t -> p (n t)"), ACT.Identity,
                                     bias=modT[:, 3, b:b + 1], scale=modT[:, 4, b:b + 1]).then_inc(h2t_ready, 1)
            act.wait_ge(shifted, 1)
            nc.scalar.activation(lg[:, :, :], lg[:, :, :], ACT.Exp).then_inc(exp_ready, 1)
            for b in range(NB):
                act.wait_ge(gathered, b + 1)
                nc.scalar.activation(exT[:, b, :], dBu[b][:, :], ACT.Identity,
                                     bias=modT[:, 3, b:b + 1], scale=modT[:, 4, b:b + 1]).then_inc(ext_ready, 1)
            for q in range(NPAIR):
                for e in (2 * q, 2 * q + 1):
                    act.wait_ge(up_ready, e + 1)
                    if e >= 4:
                        act.wait_ge(down_ready, (e - 4) // 2 + 1)
                    for c in range(FC):
                        last = nc.scalar.activation(hid[:, e % 4, c * P:(c + 1) * P], dBu[e % 2][:, c * P:(c + 1) * P],
                                                    ACT.Gelu_apprx_tanh, bias=b1c[:, e, c:c + 1])
                    last.then_inc(gelu_ready, 1)
                act.wait_ge(turned, 2 * q + 1)
                b, qq = divmod(2 * q, NPAIR)
                nc.scalar.activation(onehotT[:, b, qq, :, :], yT[:, 0], ACT.Copy).then_inc(kept_act, 1)

        @block.vector
        def _(dve):
            cnt = [0]

            def step(ins):
                cnt[0] += 1
                ins.then_inc(dve_step, 1)
                dve.wait_ge(dve_step, cnt[0])

            def norm_stats(src):
                for n in range(NB * NBLK):
                    last = nc.vector.bn_stats(st[:, n, :], src(n))
                step(last)
                for n in range(NB * NBLK):
                    last = nc.vector.bn_aggr(mv[:, n, :], st[:, n, :])
                step(last)
                return nc.vector.tensor_scalar(rstd[:, :], mv[:, :, 1], EPS, None, ALU.add)

            dve.wait_ge(s_x, 16)
            norm_stats(lambda n: x[:, n // NBLK, n % NBLK, :]).then_inc(s_set, 1)
            dve.wait_ge(s_w, 80)
            dve.wait_ge(s_seta, 2)
            step(nc.vector.tensor_scalar(scT[:, 1, :], cT, 0.5, None, ALU.mult))
            step(nc.vector.scalar_tensor_tensor(scT[:, 2, :], scT[:, 0, :], 1.0, scT[:, 1, :], ALU.add, ALU.mult))
            for b in range(NB):
                last = nc.vector.tensor_copy(scB[:, b, :], scT[:, 2, b:b + 1].to_broadcast([P, P]))
            last.then_inc(s_set, 1)
            dve.wait_ge(s_setg, 1)
            for n in range(NB * NBLK):
                last = nc.vector.tensor_scalar(acc[:, n // NBLK, n % NBLK, :], x[:, n // NBLK, n % NBLK, :],
                                               mv[:, n, 0:1], rstd[:, n:n + 1], ALU.subtract, ALU.mult)
            last.then_inc(s_set, 1)
            dve.wait_ge(s_setp, 1)
            step(nc.vector.tensor_copy(modT[:, :, :], pro[:, 0:6 * NB].rearrange("p (j b) -> p j b", j=6)))
            nc.vector.tensor_scalar(modT[:, 1, :], modT[:, 1, :], 1.0, None, ALU.add)
            nc.vector.tensor_scalar(modT[:, 4, :], modT[:, 4, :], 1.0, None, ALU.add).then_inc(s_set, 1)
            for dr in range(2):
                for k in range(DC):
                    nc.vector.scalar_tensor_tensor(wtap[:, dr, k, :], convw[:, dr, k, :], 0.5, inx[:, dr, :],
                                                   ALU.mult, ALU.mult)
            nc.vector.tensor_scalar(wz, wz, 0.5, None, ALU.mult)
            step(nc.vector.tensor_scalar(biasc[:, 0:NBIAS // 2], biasc[:, 0:NBIAS // 2], 0.5, None, ALU.mult))
            step(nc.vector.tensor_copy(part16[:, 0, :], biasc))
            step(nc.vector.tensor_copy(part32[:, :, 0], part16[:, 0, :]))
            step(nc.vector.tensor_tensor(part32[:, :, 2], biasc, part32[:, :, 0], ALU.subtract))
            step(nc.vector.tensor_copy(part16[:, 1, :], part32[:, :, 2]))
            step(nc.vector.tensor_copy(part32[:, :, 1], part16[:, 1, :]))
            nc.vector.tensor_tensor(part32[:, :, 2], part32[:, :, 2], part32[:, :, 1],
                                    ALU.subtract).then_inc(s_set, 1)
            nc.vector.tensor_scalar(Aneg[:, :, :, :], Aneg[:, :, :, :], -1.0, None, ALU.mult)
            dve.wait_ge(s_c, 10)
            for dr in range(2):
                for half in range(NH):
                    at = WAT["dskip"] + dr * NH + half
                    last = nc.vector.tensor_scalar(dskip[:, dr, half, :], ident[:, :], wp[:, at:at + 1], None, ALU.mult)
            last.then_inc(s_set, 1)
            dve.wait_ge(s_setp, 4)
            for i in range(2):
                last = nc.vector.tensor_copy(bias3[:, i].rearrange("p d h c -> p (d h c)"), dBu[1 + i][0:3, :])
            last.then_inc(s_set, 1)
            dve.wait_ge(s_setp, 2)
            nc.vector.tensor_copy(gtemp[:, 0, :], dBu[0][:, :]).then_inc(s_set, 1)
            dve.wait_ge(s_set, SET_GAB)
            step(nc.vector.tensor_scalar(gtemp[:, 1, :], gtemp[:, 0, :], 0.0, 2.0, ALU.is_ge, ALU.mult))
            step(nc.vector.scalar_tensor_tensor(gtemp[:, 2, :], gtemp[:, 0, :], -1.0, gtemp[:, 0, :], ALU.mult, ALU.max))
            step(nc.vector.tensor_scalar(gtemp[:, 2, :], gtemp[:, 2, :], 0.25, None, ALU.max))
            step(nc.vector.scalar_tensor_tensor(gmod[:, :, :, :].rearrange("p b g d -> p (b g d)"), gtemp[:, 1, :], -1.0,
                                                gtemp[:, 2, :], ALU.add, ALU.mult))
            for b in range(NB):
                nc.vector.tensor_tensor(g1[:, b, :], gmod[:, b, 0, :], lnw, ALU.mult)
                step(nc.vector.tensor_tensor(g0[:, b, :], gmod[:, b, 0, :], lnb, ALU.mult))
            for b in range(NB):
                last = nc.vector.tensor_tensor(x[:, b], x[:, b], g0[:, b:b + 1, :].to_broadcast([P, NBLK, D]), ALU.add)
            last.then_inc(s_set, 1)

            def item_v(kind, j, u):
                b, dr, par = unit(u)
                it = (kind, j, u)
                src = flat(bank(it))
                half, c = divmod(j, NCH)
                if kind == "X":
                    dve.wait_ge(tanh_ready, count_of(it, ("X", "Z")))
                    nc.vector.scalar_tensor_tensor(xc[par][:, half, c * CH:(c + 1) * CH], th_of(it), 1.0, src,
                                                   ALU.add, ALU.mult).then_inc(item_dve, 1)
                elif kind == "Z":
                    dve.wait_ge(tanh_ready, count_of(it, ("X", "Z")))
                    nc.vector.scalar_tensor_tensor(gz[par][:, 2 * j:2 * j + 2, :].rearrange("p n d -> p (n d)"),
                                                   th_of(it), 1.0, src, ALU.add, ALU.mult).then_inc(item_dve, 1)
                elif kind == "BT":
                    dve.wait_ge(pro_ready, NUMBER[it] + 1)
                    nc.vector.tensor_copy(bT[:, par, :, :],
                                          src[:, 0:NBLK * 2 * DS].rearrange("p (n s) -> p n s", n=NBLK)[:, :, 0:DS]
                                          ).then_inc(item_dve, 1)
                elif kind == "DT":
                    out = delta[par][:, half, c * CH:(c + 1) * CH]
                    dve.wait_ge(e_ready, dt_count(j, u))
                    nc.vector.tensor_scalar(sp_w[:, j, :], sp_e[:, j, :], 1.0, -1.0, ALU.add, ALU.add).then_inc(w_ready, 1)
                    nc.vector.tensor_scalar(out, src, 0.0, None, ALU.max).then_inc(item_dve, 1)
                elif kind == "O":
                    dst = acc[:, b, j * BPC:(j + 1) * BPC, :].rearrange("p n d -> p (n d)")
                    dve.wait_ge(pro_ready, NUMBER[it] + 1)
                    if dr == 0:
                        nc.vector.tensor_copy(dst, src).then_inc(item_dve, 1)
                    else:
                        nc.vector.tensor_tensor(dst, src, dst, ALU.add).then_inc(item_dve, 1)

            def finish_delta(j, u):
                _, _, par = unit(u)
                half, c = divmod(j, NCH)
                out = delta[par][:, half, c * CH:(c + 1) * CH]
                wait_item(dve, "DT", j, u)
                dve.wait_ge(ln_ready, dt_count(j, u))
                step(nc.vector.tensor_tensor(sp_e[:, j, :], sp_e[:, j, :], sp_w[:, j, :], ALU.add))
                nc.vector.tensor_tensor(out, out, sp_e[:, j, :], ALU.add).then_inc(delta_ready, 1)

            def scale_blocks(g):
                u, s = divmod(g, DS)
                _, _, par = unit(u)
                if s == 0:
                    wait_item(dve, "DU", 3, u)
                    wait_item(dve, "BT", 0, u)
                if g >= 2:
                    dve.wait_ge(dbu_ready, NCH * NH * (g - 1))
                for n in range(NBLK - DVE_BLOCKS, NBLK):
                    last = nc.vector.tensor_scalar(dBuT[:, g % 2, n, :], duT[par][:, n, :],
                                                   bT[:, par, n, s:s + 1], None, ALU.mult)
                last.then_inc(dbut_dve, 1)

            def scan_chunk(e, i):
                u, q = e // (DS * NH), NCH * e + i
                c = chunks(u)[i]
                if i == 0:
                    dve.wait_ge(da_ready, e + 1)
                    if e >= 3:
                        dve.wait_ge(hc_done, e - 2)
                dve.wait_ge(dbu_ready, q + 1)
                if i:
                    dve.wait_ge(scan_done, q)
                lo, hi = c * CH, (c + 1) * CH
                if u % 2 == 0:
                    init = hs[:, e % 3, lo - 1:lo] if i else 0.0
                    nc.vector.tensor_tensor_scan(hs[:, e % 3, lo:hi], dA[:, e % 3, lo:hi], dBu[q % 3][:, :],
                                                 init, ALU.mult, ALU.add).then_inc(scan_done, 1)
                else:
                    init = hs[:, e % 3, hi:hi + 1] if i else 0.0
                    nc.vector.tensor_tensor_scan(hs[:, e % 3, lo:hi][:, ::-1], dA[:, e % 3, lo:hi][:, ::-1],
                                                 dBu[q % 3][:, ::-1], init, ALU.mult, ALU.add).then_inc(scan_done, 1)

            def gate(u, half):
                _, _, par = unit(u)
                dve.wait_ge(yacc_done, NH * DS * (u + 1) - (NH - 1 - half))
                wait_item(dve, "Z", 3, u)
                at = gz[par][:, :, half * P:(half + 1) * P]
                nc.vector.tensor_tensor(at, yT[:, half], at, ALU.mult).then_inc(gate_done, 1)

            for k, j in FIRST_ITEMS:
                if k == "DU" and j == 0:
                    for i in range(4):
                        finish_delta(i, 0)
                item_v(k, j, 0)
            scale_blocks(0)
            for e in range(NT):
                g, half = divmod(e, NH)
                u, s = divmod(g, DS)
                scan_chunk(e, 0)
                if u > 0 and e % (NH * DS) in (1, 2):
                    gate(u - 1, e % (NH * DS) - 1)
                for j in finish_at(e):
                    finish_delta(j, u + 1)
                if e and ENDS[e - 1] is not None:
                    item_v(*ENDS[e - 1])
                scan_chunk(e, 1)
                if half == 0 and g + 1 < NG:
                    scale_blocks(g + 1)
            gate(NU - 1, 0)
            gate(NU - 1, 1)
            for k, j in LAST_ITEMS:
                item_v(k, j, NU - 1)

            wait_item(dve, "O", 1, NU - 1)
            norm_stats(lambda n: acc[:, n // NBLK, n % NBLK, :]).then_inc(var_ready, 1)
            dve.wait_ge(rstd_ready, 1)
            for b in range(NB):
                for n in range(NBLK):
                    r = b * NBLK + n
                    last = nc.vector.tensor_scalar(acc[:, b, n, :], acc[:, b, n, :], mv[:, r, 0:1], rstd[:, r:r + 1],
                                                   ALU.subtract, ALU.mult)
                step(last)
                step(nc.vector.tensor_tensor(acc[:, b], acc[:, b], g1[:, b:b + 1, :].to_broadcast([P, NBLK, D]), ALU.mult))
                step(nc.vector.tensor_tensor(x[:, b], x[:, b], acc[:, b], ALU.add))
            norm_stats(lambda n: x[:, n // NBLK, n % NBLK, :]).then_inc(var_ready, 1)
            dve.wait_ge(rstd_ready, 2)
            for b in range(NB):
                for n in range(NBLK):
                    r = b * NBLK + n
                    last = nc.vector.tensor_scalar(lnx[:, b, n, :], x[:, b, n, :], mv[:, r, 0:1], rstd[:, r:r + 1],
                                                   ALU.subtract, ALU.mult)
                last.then_inc(lnx_ready, 1)
            logits = pro[:, 0:NB * NBLK * E].rearrange("p (r e) -> p r e", e=E)
            dve.wait_ge(logits_ready, 1)
            step(nc.vector.tensor_reduce(lmax[:, :], logits, AX.X, ALU.max))
            nc.vector.tensor_tensor(lg[:, :, :], logits, lmax[:, :].unsqueeze(2).to_broadcast([P, NB * NBLK, E]),
                                    ALU.subtract).then_inc(shifted, 1)
            dve.wait_ge(exp_ready, 1)
            step(nc.vector.tensor_reduce(lsum[:, :], lg[:, :, :], AX.X, ALU.add))
            step(nc.vector.reciprocal(lsum[:, :], lsum[:, :]))
            for b in range(NB):
                rs = slice(b * NBLK, (b + 1) * NBLK)
                last = nc.vector.tensor_tensor(sm[:, :, b, :], lg[:, rs, :],
                                               lsum[:, rs].unsqueeze(2).to_broadcast([P, NBLK, E]), ALU.mult)
            last.then_inc(sm_ready, 1)
            dve.wait_ge(smt_ready, 1)
            for c in range(NCH):
                last = nc.vector.tensor_copy(smT[:, c * CH:(c + 1) * CH], dBu[c][0:16, :])
            step(last)
            for r in range(TOPK // 8):
                src = smT if r == 0 else smW
                step(nc.vector.max(top8[:, r, :], src))
                step(nc.vector.match_replace(smW, top8[:, r, :], src, -1.0))
            step(nc.vector.tensor_scalar(msk, smW, 0.0, None, ALU.is_lt))
            dve.wait_ge(ones_ready, 1)
            step(nc.vector.tensor_tensor_scan(pos, onesr, msk, 0.0, ALU.mult, ALU.add))
            nc.vector.tensor_tensor(pos, pos, msk, ALU.mult).then_inc(pos_ready, 1)
            dve.wait_ge(post_ready, 1)
            step(nc.vector.tensor_copy(posT[:, :, :, :].rearrange("p n b e -> p (n b e)"), pro[:, 0:NB * NBLK * E]))
            for b in range(NB):
                for n in range(NBLK):
                    last = nc.vector.tensor_tensor(onehot[:, b, n, :].rearrange("p (e k) -> p e k", e=E),
                                                   posT[:, n, b, :].unsqueeze(2).to_broadcast([P, E, TOPK]),
                                                   iotak[:, :].unsqueeze(1).to_broadcast([P, E, TOPK]), ALU.is_equal)
                last.then_inc(onehot_ready, 1)
            dve.wait_ge(gsel_ready, 1)
            gsel = pro[:, 0:NB * NPAIR * E].rearrange("p (b q e) -> p b q e", b=NB, q=NPAIR)
            for b in range(NB):
                last = nc.vector.tensor_tensor(gtmp[:, b], gsel[:, b], emask[:, :, :], ALU.mult)
            step(last)
            nc.vector.tensor_reduce(gcol[:, :, :], gtmp[:, :, :, :], AX.X, ALU.add).then_inc(gcol_ready, 1)
            dve.wait_ge(gcol_ready, 1)

            def keep_down(q):
                dve.wait_ge(down_ready, q + 1)
                src = dBu[2] if q % 2 == 0 else pro
                for b in range(NB):
                    last = nc.vector.scalar_tensor_tensor(eo[:, b, q, :], src[:, b * D:(b + 1) * D], gcol[:, b, q:q + 1],
                                                          gmod[:, b, 1, :], ALU.mult, ALU.mult)
                last.then_inc(eo_ready, 1)

            for q in range(NPAIR):
                dve.wait_ge(turned, 2 * q + 2)
                b, qq = divmod(2 * q + 1, NPAIR)
                nc.vector.tensor_copy(onehotT[:, b, qq, :, :], yT[:, 1]).then_inc(kept_dve, 1)
                if q:
                    keep_down(q - 1)
            keep_down(NPAIR - 1)
            for b in range(NB):
                dve.wait_ge(scattered, b + 1)
                nc.vector.tensor_tensor(x[:, b], yT[:, b], x[:, b], ALU.add).then_inc(x2_ready, 1)

        @block.tensor
        def _(pe):
            def mm(out, lhsT, rhs, start, stop):
                return nc.tensor.matmul(out, lhsT, rhs, start=start, stop=stop, skip_group_check=True)

            def turn(out, in_, start, idn=None):
                return nc.tensor.matmul(out, in_, ident[:, :] if idn is None else idn, start=start, stop=True,
                                        is_transpose=True, skip_group_check=True)

            pe.wait_ge(s_w, 80)
            pe.wait_ge(s_c, 10)
            pe.wait_ge(s_set, 2)
            for j in range(6):
                last = mm(pro[:, NB * j:NB * (j + 1)], wmod[:, j * D:(j + 1) * D], scT[:, 2, :], True, True)
            last.then_inc(s_setp, 1)
            for b in range(NB):
                for i, j in enumerate((2, 5)):
                    last = mm(dBu[0][:, (2 * b + i) * D:(2 * b + i + 1) * D], scB[:, b, :],
                              wmod[:, j * D:(j + 1) * D], True, True)
            last.then_inc(s_setp, 1)
            pe.wait_ge(s_set, 3)
            for b in range(NB):
                for n in range(NBLK):
                    last = turn(yT[:, b, n, :], acc[:, b, n, :], True)
            last.then_inc(s_setp, 1)
            pe.wait_ge(s_set, SET_PARTS)
            for i in range(2):
                for k in range(NBIAS // 2):
                    last = turn(dBu[1 + i][0:3, k * P:(k + 1) * P], part32[:, i * NBIAS // 2 + k, :], True)
            last.then_inc(s_setp, 1)
            pe.wait_ge(s_seta, 4)
            pe.wait_ge(s_set, SET_DONE)

            def item_t(it, part):
                kind, j, u = it
                b, dr, par = unit(u)
                n_it = NUMBER[it]
                dst = flat(bank(it))
                half, c = divmod(j, NCH)
                if part == 0 and n_it >= 5:
                    wait_item(pe, *ORDER[n_it - 5 if n_it < NFIRST else n_it - 1])
                    if n_it == NFIRST:
                        for k in range(2, 6):
                            wait_item(pe, *ORDER[n_it - k])
                if kind == "X":
                    at = c * CH + (part if dr == 0 else 2 * PAD - part)
                    last = mm(dst, wtap[:, dr, part, half * P:(half + 1) * P], hT[:, b, at:at + CH], part == 0, False)
                    if part == DC - 1:
                        last = mm(dst, bias3[:, 0, dr, half, :], ones3[:, 0:1].to_broadcast([3, CH]), False, True)
                elif kind == "Z":
                    at = PAD + (2 * j + part) * P
                    last = mm(dst[:, part * DI:(part + 1) * DI], hT[:, b, at:at + P], wz[:, dr, :], True, True)
                elif kind == "B":
                    if part == 0:
                        for h in range(NH):
                            wait_item(pe, "X", h * NCH + j, u)
                    last = mm(dst[0:XD, :], xproj[:, dr, part, :], xc[par][:, part, j * CH:(j + 1) * CH],
                              part == 0, part == NH - 1)
                elif kind == "BT":
                    if part == 0:
                        wait_item(pe, "B", 1, u)
                    for n in range(part * BPC, (part + 1) * BPC):
                        last = turn(dst[:, n * 2 * DS:(n + 1) * 2 * DS], xdbl[DR:XD, n * P:(n + 1) * P], True,
                                    ident[DR:XD, DR:XD])
                elif kind == "DT":
                    if part == 0:
                        last = mm(dst, dtw[:, dr, half * P:(half + 1) * P], xdbl[0:DR, c * CH:(c + 1) * CH], True, False)
                    else:
                        last = mm(dst, bias3[:, 1, dr, half, :], ones3[:, 0:1].to_broadcast([3, CH]), False, True)
                elif kind == "DU":
                    if part == 0:
                        pe.wait_ge(du_ready, dt_count(j, u))
                    for i in (2 * part, 2 * part + 1):
                        last = turn(dst[:, i * P:(i + 1) * P], sp_w[:, j, i * P:(i + 1) * P], True)
                elif kind == "YT":
                    if part == 0:
                        pe.wait_ge(gate_done, NH * (u + 1))
                    for i in (2 * part, 2 * part + 1):
                        last = turn(dst[:, i * P:(i + 1) * P], gz[par][:, c * BPC + i, half * P:(half + 1) * P], True)
                elif kind == "O":
                    if part == 0:
                        wait_item(pe, "YT", 3, u)
                    for i in (2 * part, 2 * part + 1):
                        n = j * BPC + i
                        o = dst[:, i * D:(i + 1) * D]
                        if dr == 0:
                            turn(o, hT[:, b, PAD + n * P:PAD + (n + 1) * P], True)
                        for h in range(NH):
                            last = mm(o, yg[:, h, n * P:(n + 1) * P], outproj[:, dr, h, :],
                                      dr == 1 and h == 0, h == NH - 1)
                if part == parts_of(kind) - 1:
                    last.then_inc(pro_ready, 1)

            def dbu_chunk(e, i):
                u, half = e // (DS * NH), e % NH
                g, q = e // NH, NCH * e + i
                c = chunks(u)[i]
                if half == 0 and i == 0:
                    pe.wait_ge(dbut_act, g + 1)
                    pe.wait_ge(dbut_dve, g + 1)
                if q >= 3:
                    pe.wait_ge(scan_done, q - 2)
                for k in range(BPC):
                    last = turn(dBu[q % 3][:, k * P:(k + 1) * P],
                                dBuT[:, g % 2, c * BPC + k, half * P:(half + 1) * P], True)
                last.then_inc(dbu_ready, 1)

            def y_start(u, half):
                _, dr, par = unit(u)
                if u > 0:
                    pe.wait_ge(gate_done, NH * (u - 1) + half + 1)
                for n in range(NBLK):
                    mm(yT[:, half, n, :], xc[par][:, half, n * P:(n + 1) * P], dskip[:, dr, half, :],
                       n % BPC == 0, True)

            def y_add(e):
                half = e % NH
                pe.wait_ge(hc_done, e + 1)
                for n in range(NBLK):
                    last = turn(yT[:, half, n, :], hc[:, e % 3, n * P:(n + 1) * P], False)
                last.then_inc(yacc_done, 1)

            for k, j in FIRST_ITEMS:
                for part in range(parts_of(k)):
                    item_t((k, j, 0), part)
            for i in range(NCH):
                dbu_chunk(0, i)
            for e in range(NT):
                u, t = divmod(e, DS * NH)
                if OP == 0:
                    for i in range(NCH):
                        if e + 1 < NT:
                            dbu_chunk(e + 1, i)
                        if i < len(PARTS[e]):
                            item_t(*PARTS[e][i])
                elif OP in (1, 2):
                    for i in range(NCH):
                        if e + 1 < NT:
                            dbu_chunk(e + 1, i)
                    if OP == 2:
                        for p in PARTS[e]:
                            item_t(*p)
                if t in (2, 3):
                    y_start(u, t - 2)
                if e >= 2:
                    y_add(e - 2)
                if OP == 1:
                    for p in PARTS[e]:
                        item_t(*p)
            y_add(NT - 2)
            y_add(NT - 1)
            for k, j in LAST_ITEMS:
                for part in range(parts_of(k)):
                    item_t((k, j, NU - 1), part)

            for b in range(NB):
                pe.wait_ge(lnx_ready, b + 1)
                for n in range(NBLK):
                    last = turn(yT[:, b, n, :], lnx[:, b, n, :], True)
                last.then_inc(lnt_ready, 1)
            for b in range(NB):
                pe.wait_ge(h2t_ready, b + 1)
                for n in range(NBLK):
                    r = b * NBLK + n
                    last = mm(pro[:, r * E:(r + 1) * E], lnT[:, b, n * P:(n + 1) * P], w("wg"), True, True)
            last.then_inc(logits_ready, 1)
            pe.wait_ge(sm_ready, 1)
            for n in range(NBLK):
                c, i = divmod(n, BPC)
                last = turn(dBu[c][0:16, i * P:(i + 1) * P], sm[:, n, :, :].rearrange("p b e -> p (b e)"), True)
            last.then_inc(smt_ready, 1)
            pe.wait_ge(pos_ready, 1)
            for n in range(NBLK):
                last = turn(pro[:, n * 16:(n + 1) * 16], pos[:, n * P:(n + 1) * P], True, ident[0:16, 0:16])
            last.then_inc(post_ready, 1)
            for b in range(NB):
                pe.wait_ge(onehot_ready, b + 1)
                for n in range(NBLK):
                    last = mm(dBu[b][:, :], lnx[:, b, n, :], onehot[:, b, n, :], n == 0, n == NBLK - 1)
                last.then_inc(gathered, 1)
            for b in range(NB):
                for q in range(NPAIR):
                    at = (b * NPAIR + q) * E
                    for n in range(NBLK):
                        last = mm(pro[:, at:at + E], onehot[:, b, n, q * P:(q + 1) * P], sm[:, n, b, :],
                                  n == 0, n == NBLK - 1)
            last.then_inc(gsel_ready, 1)
            pe.wait_ge(s_w1, 16)
            pe.wait_ge(s_w2, 32)

            def up(e):
                if e < 2:
                    pe.wait_ge(ext_ready, NB)
                else:
                    pe.wait_ge(gelu_ready, e - 1)
                for c in range(FC):
                    last = mm(dBu[e % 2][:, c * P:(c + 1) * P], w1s[:, e, c * P:(c + 1) * P],
                              exT[:, :, e * TOPK:(e + 1) * TOPK], True, True)
                last.then_inc(up_ready, 1)

            def down(q):
                pe.wait_ge(gelu_ready, 2 * q + 2)
                if q == 1:
                    pe.wait_ge(gcol_ready, 1)
                if q >= 2:
                    pe.wait_ge(eo_ready, q - 1)
                dst = dBu[2] if q % 2 == 0 else pro
                for b in range(NB):
                    for i in range(2):
                        e = 2 * q + i
                        o = dst[i * TOPK:(i + 1) * TOPK, b * D:(b + 1) * D]
                        for c in range(FC):
                            mm(o, hid[:, e % 4, c * P + b * TOPK:c * P + (b + 1) * TOPK], w2s[:, e, c, :], c == 0, False)
                        last = mm(o, ones[:, 0:TOPK], b2r[:, e, :], False, True)
                last.then_inc(down_ready, 1)

            def turn_onehot(m):
                b, q = divmod(m, NPAIR)
                if m >= 2:
                    pe.wait_ge(kept_act if m % 2 == 0 else kept_dve, m // 2)
                for n in range(NBLK):
                    last = turn(yT[:, m % 2, n, :], onehot[:, b, n, q * P:(q + 1) * P], True)
                last.then_inc(turned, 1)

            for q in range(NPAIR):
                up(2 * q)
                up(2 * q + 1)
                turn_onehot(2 * q)
                turn_onehot(2 * q + 1)
                if q:
                    down(q - 1)
            down(NPAIR - 1)
            pe.wait_ge(kept_act, NPAIR)
            pe.wait_ge(kept_dve, NPAIR)
            pe.wait_ge(eo_ready, NPAIR)
            for b in range(NB):
                for n in range(NBLK):
                    for q in range(NPAIR):
                        last = mm(yT[:, b, n, :], onehotT[:, b, q, n, :], eo[:, b, q, :], q == 0, q == NPAIR - 1)
                last.then_inc(scattered, 1)




def kernel(**inputs):
    import concourse.bacc as bacc
    from concourse.bass_utils import run_bass_kernel_spmd

    a = {k: np.asarray(v) for k, v in inputs.items()}

    def both(name, lay):
        return [lay(a[f"L0_attn_{name}_{d}"]) for d in "fb"]

    def halves(m):
        return m.reshape(NH, P, -1).transpose(1, 0, 2).reshape(P, -1)

    wpack = np.concatenate(
        both("A_log", halves) + both("D", halves)
        + both("in_proj", lambda m: m[:DI].T) + both("in_proj", lambda m: m[DI:].T)
        + both("x_proj", lambda m: halves(m.T)) + both("out_proj", lambda m: halves(m.T))
        + [a["L0_ffn_Wg"].T, a["L0_ffn_b1"].reshape(E, FC, P).transpose(2, 0, 1).reshape(P, -1)]
        + both("conv_b", halves) + both("dt_b", halves), axis=1)
    bcast = np.concatenate(both("conv_w", lambda m: m.T.reshape(-1)) + [a["L0_attn_ln_w"], a["L0_attn_ln_b"]])
    dtw = np.stack(both("dt_w", lambda m: m.T), axis=1)
    arrays = {"x_in": a["L0_attn_x"], "mod_in": np.concatenate([a["L0_c"].T, a["L0_wmod"]], axis=1), "wpack_in": wpack, "bcast_in": bcast, "dtw_in": dtw,
              "w1_in": a["L0_ffn_W1"], "w2_in": a["L0_ffn_W2"], "b2_in": a["L0_ffn_b2"]}
    arrays = {k: np.ascontiguousarray(v) for k, v in arrays.items()}

    nc = bacc.Bacc("TRN2", target_bir_lowering=False, num_devices=1)
    aps = [nc.dram_tensor(k, v.shape, mybir.dt.from_np(v.dtype), kind="ExternalInput").ap() for k, v in arrays.items()]
    crow = nc.dram_tensor("c_rows", (NU, DS, L), mybir.dt.float32, kind="Internal").ap()
    out = nc.dram_tensor("out", (NB, L, D), mybir.dt.float32, kind="ExternalOutput").ap()
    build_block(nc, *aps, crow, out)
    r = run_bass_kernel_spmd(nc, [arrays], core_ids=[0])
    return r.results[0]["out"]
```

```python
import numpy as np
import concourse.bass as bass
from concourse import mybir
from contextlib import ExitStack

NB, L, D = 2, 1024, 128
DI, DS, DC, DR = 256, 16, 4, 64
E, TOPK, F = 8, 64, 512
P = 128
NH = DI // P
NBLK = L // P
CH = 512
NCH = L // CH
BPC = CH // P
XD = DR + 2 * DS
NU = 2 * NB
NG = NU * DS
NT = NG * NH
PAD = DC - 1
FC = F // P
NPAIR = E // 2
EPS = 1e-5

NBIAS = 2 * NH

WPARTS = [("a_log", 2 * NH * DS), ("dskip", 2 * NH),
          ("in_x", 2 * DI), ("in_z", 2 * DI), ("xproj", 2 * NH * XD), ("outproj", 2 * NH * D),
          ("wg", E), ("b1", E * FC), ("b2", E), ("bias", 2 * NBIAS)]
WAT, WCOLS = {}, 0
for _name, _n in WPARTS:
    WAT[_name] = WCOLS
    WCOLS += _n
CONVW_COLS = 2 * DC * DI

DVE_BLOCKS, DVE_BLOCKS_SOFTPLUS, DVE_BLOCKS_LAST = 3, 4, 2
SP_FROM, SP_TO = 9, 13


def dve_blocks(g):
    u, s = divmod(g, DS)
    if u + 1 == NU:
        return DVE_BLOCKS_LAST
    return DVE_BLOCKS_SOFTPLUS if SP_FROM <= s < SP_TO else DVE_BLOCKS


FIRST_ITEMS = ([("X", 0), ("X", 2), ("X", 1), ("X", 3), ("B", 0), ("B", 1), ("BT", 0)]
               + [("DT", j) for j in range(4)] + [("DU", j) for j in range(4)])
LAST_ITEMS = [("YT", j) for j in range(4)] + [("O", j) for j in range(2)]
NORM_ITEMS = [("LT", 0), ("LT", 1), ("LG", 0), ("ST", 0), ("ST", 1), ("PT", 0)]
NORM_AT = {8: 0, 9: 1, 11: 2, 12: 3, 13: 4, 14: 5, 15: 6, 30: 7}
POW_AT = (9, 15)
NORM_ITEM_AT = {("LT", 0): 0, ("LT", 1): 1, ("LG", 0): 3, ("ST", 0): 7, ("ST", 1): 8, ("PT", 0): 31}
SOFTMAX_AT, CHOOSE_AT, SLOTS_AT = 6, 10, 28
CHOOSE_STEPS = [t for t in range(CHOOSE_AT, SLOTS_AT) if t % 9 != 0]
assert len(CHOOSE_STEPS) == 2 * (TOPK // 8)


def parts_of(kind):
    return 4 if kind == "X" else 2


def schedule():
    parts = [[] for _ in range(NT)]
    for u in range(NU):
        items = []
        if u + 1 < NU:
            items += [("X", 0, u + 1)]
            items += [(k, j, u - 1) for k, j in LAST_ITEMS] if u > 0 else [("Z", j, u) for j in range(4)]
            items += [("X", j, u + 1) for j in range(1, 4)]
            items += [("B", 0, u + 1), ("B", 1, u + 1), ("BT", 0, u + 1)]
            items += [("DT", j, u + 1) for j in range(4)] + [("Z", j, u + 1) for j in range(4)]
            items += [("DU", j, u + 1) for j in range(4)]
        at = NH * DS * u
        for it in items:
            for p in range(0, parts_of(it[0]), 2):
                parts[at] += [(it, p), (it, p + 1)]
                at += 1
        assert at <= NH * DS * (u + 1) - 2
    at = NH * DS * (NU - 1)
    for (k, j), t in NORM_ITEM_AT.items():
        parts[at + t] += [((k, j, 0), 0), ((k, j, 0), 1)]
    for k, j in LAST_ITEMS:
        t = min(t for t in range(3, NH * DS) if not parts[at + t])
        parts[at + t] += [((k, j, NU - 2), 0), ((k, j, NU - 2), 1)]
    ends = [[it for it, p in row if p == parts_of(it[0]) - 1] for row in parts]
    return parts, [row[0] if row else None for row in ends]


PARTS, ENDS = schedule()
LN_AT = 22
ORDER = [(k, j, 0) for k, j in FIRST_ITEMS]
ORDER += [it for it in ENDS if it is not None]
NLAST = len(ORDER)
ORDER += [(k, j, NU - 1) for k, j in LAST_ITEMS] + [(k, j, 1) for k, j in NORM_ITEMS]
NUMBER = {it: n for n, it in enumerate(ORDER)}
NFIRST = len(FIRST_ITEMS)
BY_ACT = ("B", "DU", "YT", "LT")
BY_DVE = ("X", "Z", "BT", "DT", "O", "LG", "ST", "PT")


def count_of(it, kinds):
    return sum(o[0] in kinds for o in ORDER[:NUMBER[it] + 1])


def finish_at(e):
    u, t = divmod(e, DS * NH)
    if u + 1 == NU or t not in (LN_AT + 1, LN_AT + 2):
        return ()
    return (0, 1) if t == LN_AT + 1 else (2, 3)


def build_block(nc, x_d, mod_d, wpack_d, bcast_d, dtw_d, w1_d, w2_d, crow_d, out_d):
    fp32 = mybir.dt.float32
    ALU = mybir.AluOpType
    ACT = mybir.ActivationFunctionType
    AX = mybir.AxisListType
    ctx = ExitStack()
    with ctx:
        def sb(name, shape):
            return ctx.enter_context(nc.sbuf_tensor(name, shape, fp32))

        def pb(name, shape):
            return ctx.enter_context(nc.psum_tensor(name, shape, fp32))

        def sem(name):
            return ctx.enter_context(nc.semaphore(name))

        x = sb("x", [P, NB, NBLK, D])
        acc = sb("acc", [P, NB, NBLK, D])
        hT = sb("hT", [P, NB, L + 2 * PAD])
        wp = sb("wp", [P, WCOLS])
        bias3 = ctx.enter_context(nc.sbuf_tensor("bias3", [3, 2, NH, P], mybir.dt.bfloat16))
        ones3 = ctx.enter_context(nc.sbuf_tensor("ones3", [3, 1], mybir.dt.bfloat16))
        part16 = ctx.enter_context(nc.sbuf_tensor("part16", [P, 2, NBIAS], mybir.dt.bfloat16))
        part32 = sb("part32", [P, NBIAS, 3])
        lnv = sb("lnv", [P, 2, D])
        dtw = sb("dtw", [DR, 2, DI])
        area1 = sb("area1", [P, 2, 2, NH, L])
        xc = [area1[:, p, 0] for p in range(2)]
        delta = [area1[:, p, 1] for p in range(2)]
        area2 = sb("area2", [P, 2, 2, NBLK, DI])
        duT = [area2[:, p, 0] for p in range(2)]
        gz = [area2[:, p, 1] for p in range(2)]
        bT = sb("bT", [P, 2, NBLK, DS])
        sp_e = sb("sp_e", [P, NH * NCH, CH])
        xdbl = sb("xdbl", [XD, L])
        th = sb("th", [P, CH])
        dA = sb("dA", [P, 3, L])
        dBuT = sb("dBuT", [P, 2, NBLK, DI])
        hc = sb("hc", [P, 3, L])
        area3 = sb("area3", [P, 6 + NH, L])
        hs = area3[:, 0:3, :]
        Cb = area3[:, 3:6, :]
        yg = area3[:, 6:6 + NH, :]
        sp_w = yg.rearrange("p h (c n) -> p (h c) n", c=NCH)
        wtap = sb("wtap", [P, 2, DC, DI])
        Aneg = sb("Aneg", [P, 2, NH, DS])
        dskip = sb("dskip", [P, 2, NH, P])
        ident = sb("ident", [P, P])
        ones = sb("ones", [1, P])
        scT = sb("scT", [P, 4, NB])
        modT = sb("modT", [P, 6, NB])
        g0 = sb("g0", [P, NB, D])
        g1 = sb("g1", [P, NB, D])
        b2g = sb("b2g", [P, NB, E])
        st = sb("st", [P, NB * NBLK, 6])
        mv = sb("mv", [P, NB * NBLK, 2])
        rstd = sb("rstd", [P, NB * NBLK])
        mhalf = sb("mhalf", [P, NB * NBLK])

        yT = pb("yT", [P, NH, NBLK, P])
        dBu = [pb(f"dBu{i}", [P, CH]) for i in range(3)]
        pro = pb("pro", [P, CH])

        def bank(it):
            n = NUMBER[it]
            if n >= NLAST:
                return [pro, dBu[1]][(n - NLAST) % 2]
            if n < NFIRST:
                return [pro, yT[:, 0, 0:BPC], yT[:, 0, BPC:NBLK], yT[:, 1, 0:BPC], yT[:, 1, BPC:NBLK]][n % 5]
            return pro

        def flat(b):
            return b[:, :] if len(b.shape) == 2 else b.rearrange("p n t -> p (n t)")

        def th_of(it):
            return th[:, :] if NUMBER[it] >= NFIRST else hs[:, 0, (NUMBER[it] % 2) * CH:(NUMBER[it] % 2 + 1) * CH]

        s_x = sem("x_loaded")
        s_w = sem("weights_loaded")
        s_m = sem("modulation_loaded")
        s_v = sem("ln_and_dt_weights_loaded")
        s_c = sem("consts_ready")
        xvar_ready = sem("xvar_ready")
        xrstd_ready = sem("xrstd_ready")
        tanhc_ready = sem("tanhc_ready")
        aexp_ready = sem("aexp_ready")
        siluc_ready = sem("siluc_ready")
        mod_ready = sem("mod_ready")
        gab_ready = sem("gab_ready")
        modt_ready = sem("modt_ready")
        xn_ready = sem("xn_ready")
        xn_turned = sem("xn_turned")
        ht_ready = sem("ht_ready")
        parts_ready = sem("bias_parts_ready")
        parts_turned = sem("bias_parts_turned")
        weights_ready = sem("weights_ready")
        bias_ready = sem("bias_ready")
        gab_kept = sem("gab_kept")
        pro_ready = sem("pro_ready")
        item_act = sem("item_act")
        item_dve = sem("item_dve")
        tanh_ready = sem("tanh_ready")
        ln_ready = sem("ln_ready")
        e_ready = sem("e_ready")
        w_ready = sem("w_ready")
        r_ready = sem("r_ready")
        delta_ready = sem("delta_ready")
        du_ready = sem("du_ready")
        c_stored = sem("c_stored")
        cb_ready = [sem(f"cb_ready{i}") for i in range(3)]
        da_ready = sem("da_ready")
        dbut_act = sem("dbut_act")
        dbut_dve = sem("dbut_dve")
        dbu_ready = sem("dbu_ready")
        scan_done = sem("scan_done")
        hc_done = sem("hc_done")
        yacc_done = sem("yacc_done")
        gate_done = sem("gate_done")
        act_step = sem("act_step")
        dve_step = sem("dve_step")
        var_ready = sem("var_ready")
        rstd_ready = sem("rstd_ready")
        lnx_ready = sem("lnx_ready")
        exp_ready = sem("exp_ready")
        sm_ready = sem("sm_ready")
        ones_ready = sem("ones_ready")
        pos_ready = sem("pos_ready")
        onehot_ready = sem("onehot_ready")
        gathered = sem("gathered")
        ext_ready = sem("ext_ready")
        slogits_ready = sem("slogits_ready")
        slots_shifted = sem("slots_shifted")
        slots_exp = sem("slots_exp")
        eot_ready = sem("eot_ready")
        eo_turned = sem("eo_turned")
        gcol_ready = sem("gcol_ready")
        up_ready = sem("up_ready")
        gelu_ready = sem("gelu_ready")
        turned = sem("onehot_turned")
        kept_act = sem("onehot_kept_act")
        kept_dve = sem("onehot_kept_dve")
        down_ready = sem("down_ready")
        eo_ready = sem("eo_ready")
        scattered = sem("scattered")
        x2_ready = sem("x2_ready")
        s_w1 = sem("w1_loaded")
        s_w2 = sem("w2_loaded")
        s_out = sem("out_stored")

        def w(name, n=None):
            return wp[:, WAT[name]:WAT[name] + (dict(WPARTS)[name] if n is None else n)]

        def down_bank(q):
            return dBu[0] if q % 2 == 0 else dBu[2]

        def up_bank(q):
            return flat(yT[:, 0, q % 2 * BPC:(q % 2 + 1) * BPC])

        def dtb(dr, half):
            at = WAT["bias"] + NBIAS + dr * NH + half
            return wp[:, at:at + 1]

        def unit(u):
            return u // 2, u % 2, u % 2

        def wait_item(eng, *it):
            if it[0] in BY_ACT:
                eng.wait_ge(item_act, count_of(it, BY_ACT))
            else:
                eng.wait_ge(item_dve, count_of(it, BY_DVE))

        def chunks(u):
            return range(NCH) if u % 2 == 0 else range(NCH - 1, -1, -1)

        def dt_count(j, u):
            return 4 * u + j + 1

        inx = w("in_x").rearrange("p (d c) -> p d c", d=2)
        wz = w("in_z").rearrange("p (d c) -> p d c", d=2)
        xproj = w("xproj").rearrange("p (d h c) -> p d h c", d=2, h=NH)
        outproj = w("outproj").rearrange("p (d h c) -> p d h c", d=2, h=NH)
        convrow = hc[:, 0:2, :].rearrange("p a b -> p (a b)")
        convw = convrow.rearrange("p (d k c) -> p d k c", d=2, k=DC)
        gtemp = area3[:, 1, 0:3 * NB * D].rearrange("p (i s) -> p i s", i=3)
        scB = area3[:, 5, 0:NB * P].rearrange("p (b d) -> p b d", b=NB)
        lnw, lnb = lnv[:, 0, :], lnv[:, 1, :]
        modp = area3[:, 4, 0:NB + 6 * D]
        cT, wmod = modp[:, 0:NB], modp[:, NB:NB + 6 * D]
        biasc = w("bias", NBIAS)
        b1c = w("b1").rearrange("p (e c) -> p e c", e=E)

        onehot = area1[:, :, :, :, :].rearrange("p a b c d -> p (a b c d)").rearrange(
            "p (b n s) -> p b n s", b=NB, n=NBLK)
        onehotT = area2[:, :, :, :, :].rearrange("p a b c d -> p (a b c d)").rearrange(
            "p (b q n t) -> p b q n t", b=NB, q=NPAIR, n=NBLK)
        w1s = dBuT[:, :, :, :].rearrange("p a b c -> p (a b c)").rearrange("p (e f) -> p e f", e=E)
        w2a = wtap[:, :, :, :].rearrange("p a b c -> p (a b c)").rearrange("p (e c h) -> p e c h", e=4, c=FC)
        w2b = hT[:, 0, 0:2 * F].rearrange("p (e c h) -> p e c h", e=2, c=FC)
        w2c = acc[:, 0, :, :].rearrange("p n d -> p (n d)").rearrange("p (e c h) -> p e c h", e=2, c=FC)
        w2s = [w2a[:, e] for e in range(4)] + [w2b[:, e] for e in range(2)] + [w2c[:, e] for e in range(2)]
        lnT = hT[:, :, 0:L]
        exT = hc[:, 2, :].rearrange("p (b s) -> p b s", b=NB)
        hid = hc[:, 1, :].rearrange("p (q i c k) -> p q i c k", q=2, i=2, c=FC)
        smT = xdbl[0:E, :]
        rows8 = [area2[0:E, b, 0].rearrange("p n d -> p (n d)") for b in range(NB)]
        smW = [rows8[b][:, 0:L] for b in range(NB)]
        onesr = [rows8[b][:, L:2 * L] for b in range(NB)]
        eo = area3[:, 3, :].rearrange("p (b q h) -> p b q h", b=NB, q=NPAIR)
        lnx = sp_e[:, :, :].rearrange("p (b m) (n d) -> p b (m n) d", b=NB, n=BPC)
        eoT = hc[:, 0, 0:CH].rearrange("p (e k) -> p e k", e=E)
        slg = hc[:, 0, CH:CH + NB * NPAIR * E].rearrange("p (b q e) -> p b q e", b=NB, q=NPAIR)
        smax = hc[:, 0, CH + P:CH + P + NB * NPAIR].rearrange("p (b q) -> p b q", b=NB)
        lg = th[:, 0:P].rearrange("p (r e) -> p r e", e=E)
        lmax = sb("lmax", [P, NB * NBLK])
        lsum = sb("lsum", [P, NB * NBLK])
        sm = th[:, P:2 * P].rearrange("p (b n e) -> p b n e", n=NBLK, b=NB)
        posT = th[:, 2 * P:3 * P].rearrange("p (b n e) -> p b n e", n=NBLK, b=NB)
        iotak = sb("iotak", [P, TOPK])
        emask = sb("emask", [P, NPAIR, E])
        gcol = sb("gcol", [P, NB, NPAIR])
        gtmp = th[:, 3 * P:3 * P + NB * NPAIR * E].rearrange("p (b q e) -> p b q e", b=NB, q=NPAIR)
        top8 = sb("top8", [E, TOPK // 8, 8])

        block = ctx.enter_context(nc.Block())

        @block.sync
        def _(sp):
            def load_x(b):
                sp.dma_start(x[:, b], x_d[b].rearrange("(n p) d -> p n d", p=P)).then_inc(s_x, 16)

            load_x(0)
            sp.dma_start(modp, mod_d).then_inc(s_m, 16)
            sp.dma_start(wp[:, :], wpack_d).then_inc(s_w, 16)
            sp.dma_start(convrow, bcast_d[0:CONVW_COLS].partition_broadcast(P)).then_inc(s_w, 16)
            sp.dma_start(lnv[:, :, :].rearrange("p a b -> p (a b)"),
                         bcast_d[CONVW_COLS:CONVW_COLS + 2 * D].partition_broadcast(P)).then_inc(s_v, 16)
            sp.dma_start(dtw[:, :, :], dtw_d).then_inc(s_v, 16)
            sp.wait_ge(s_x, 16)
            load_x(1)
            for g in range(NG):
                u, s = divmod(g, DS)
                if s == 0:
                    wait_item(sp, "B", 1, u)
                    sp.dma_start(crow_d[u], xdbl[DR + DS:XD, :]).then_inc(c_stored, 16)
                    sp.wait_ge(c_stored, 16 * (u + 1))
                if g >= 3:
                    sp.wait_ge(hc_done, NH * (g - 2))
                if g == NG - DS // 2:
                    wait_item(sp, "X", 3, NU - 1)
                    sp.wait_ge(var_ready, 2)
                    wait_item(sp, "LG", 0, 0)
                    for dst, lo, hi in ((w2a, 0, 4), (w2b, 4, 6), (w2c, 6, 8)):
                        sp.dma_start(dst, w2_d[lo:hi].rearrange("e (c p) h -> p e c h", p=P)).then_inc(s_w2, 16)
                sp.dma_start(Cb[:, g % 3, :], crow_d[u, s:s + 1, :].partition_broadcast(P)).then_inc(cb_ready[g % 3], 16)
            sp.wait_ge(dbu_ready, NCH * NT)
            sp.dma_start(w1s, w1_d.rearrange("e h f -> h e f")).then_inc(s_w1, 16)
            for b in range(NB):
                for c in range(NCH):
                    ns = slice(c * BPC, (c + 1) * BPC)
                    sp.wait_ge(x2_ready, NCH * b + c + 1)
                    sp.dma_start(out_d[b].rearrange("(n p) d -> p n d", p=P)[:, ns, :], x[:, b, ns, :]).then_inc(s_out, 16)
            sp.wait_ge(s_out, 16 * NB * NCH)

        @block.gpsimd
        def _(g_):
            g_.memset(ident[:, :], 0.0).then_inc(s_c, 1)
            g_.memset(ones[:, :], 1.0).then_inc(s_c, 1)
            g_.memset(mhalf[:, :], -0.5).then_inc(s_c, 1)
            g_.memset(ones3[:, :], 1.0).then_inc(s_c, 1)
            g_.memset(hT[:, :, :], 0.0).then_inc(s_c, 1)
            g_.memset(emask[:, :, :], 0.0).then_inc(s_c, 1)
            g_.iota(iotak[:, :], [[1, TOPK]], base=1, channel_multiplier=0,
                    allow_small_or_imprecise_dtypes=True).then_inc(s_c, 1)
            g_.wait_ge(s_c, 7)
            g_.affine_select(out=ident[:, :], in_=ident[:, :], compare_op=ALU.not_equal, fill=1.0, base=0,
                             pattern=[[-1, P]], channel_multiplier=1).then_inc(s_c, 1)
            g_.wait_ge(s_c, 8)
            g_.affine_select(out=emask[0:64, :, :], in_=emask[0:64, :, :], compare_op=ALU.not_equal, fill=1.0,
                             base=0, pattern=[[-2, NPAIR], [1, E]], channel_multiplier=0).then_inc(s_c, 1)
            g_.wait_ge(s_c, 9)
            g_.affine_select(out=emask[64:P, :, :], in_=emask[64:P, :, :], compare_op=ALU.not_equal, fill=1.0,
                             base=-1, pattern=[[-2, NPAIR], [1, E]], channel_multiplier=0).then_inc(s_c, 1)
            g_.wait_ge(s_c, 10)
            for b in range(NB):
                rs = slice(b * NBLK, (b + 1) * NBLK)
                g_.wait_ge(xvar_ready, b + 1)
                g_.tensor_tensor(rstd[:, rs], rstd[:, rs], mhalf[:, rs], ALU.pow).then_inc(xrstd_ready, 1)

            def pool_r(j, u):
                g_.wait_ge(w_ready, dt_count(j, u))
                g_.tensor_tensor(sp_w[:, j, :], sp_e[:, j, :], sp_w[:, j, :], ALU.subtract).then_inc(r_ready, 1)

            def pool_du(j, u):
                _, _, par = unit(u)
                half, c = divmod(j, NCH)
                g_.wait_ge(delta_ready, dt_count(j, u))
                g_.tensor_tensor(sp_w[:, j, :], delta[par][:, half, c * CH:(c + 1) * CH],
                                 xc[par][:, half, c * CH:(c + 1) * CH], ALU.mult).then_inc(du_ready, 1)

            pows = [0]

            def rstd_pow(b):
                pows[0] += 1
                g_.wait_ge(var_ready, pows[0])
                rs = slice(b * NBLK, (b + 1) * NBLK)
                g_.tensor_tensor(rstd[:, rs], rstd[:, rs], mhalf[:, rs], ALU.pow).then_inc(rstd_ready, 1)

            for j in range(4):
                pool_r(j, 0)
            for j in range(4):
                pool_du(j, 0)
            for e in range(NT):
                g = e // NH
                for j in finish_at(e):
                    pool_du(j, e // (DS * NH) + 1)
                g_.wait_ge(scan_done, NCH * (e + 1))
                g_.wait_ge(cb_ready[g % 3], 16 * (g // 3 + 1))
                if e >= 3:
                    g_.wait_ge(yacc_done, e - 2)
                g_.tensor_tensor(hc[:, e % 3, :], hs[:, e % 3, :], Cb[:, g % 3, :], ALU.mult).then_inc(hc_done, 1)
                if e >= 1 and ENDS[e - 1] is not None and ENDS[e - 1][0] == "DT":
                    pool_r(*ENDS[e - 1][1:])
                if e - NH * DS * (NU - 2) in POW_AT:
                    rstd_pow(0)
                if e == NH * DS * (NU - 1) + 2:
                    g_.memset(onesr[0], 1.0).then_inc(ones_ready, 1)

            g_.memset(onesr[1], 1.0).then_inc(ones_ready, 1)
            for n in range(2):
                rstd_pow(1)

        @block.scalar
        def _(act):
            cnt = [0]

            def then_wait(ins):
                cnt[0] += 1
                ins.then_inc(act_step, 1)
                act.wait_ge(act_step, cnt[0])

            act.wait_ge(s_m, 16)
            nc.scalar.activation(scT[:, 0, :], cT, ACT.Tanh, scale=0.5).then_inc(tanhc_ready, 1)
            act.wait_ge(s_w, 32)
            nc.scalar.activation(Aneg[:, :, :, :].rearrange("p a b c -> p (a b c)"), w("a_log"),
                                 ACT.Exp).then_inc(aexp_ready, 1)
            act.wait_ge(modt_ready, 1)
            act.wait_ge(s_c, 10)

            def modulate(b):
                act.wait_ge(xn_turned, b + 1)
                for c in range(NCH):
                    src = yT[:, 0, c * BPC:(c + 1) * BPC].rearrange("p n t -> p (n t)") if b == 0 else dBu[1 + c][:, :]
                    last = nc.scalar.activation(hT[:, b, PAD + c * CH:PAD + (c + 1) * CH], src, ACT.Identity,
                                                bias=modT[:, 0, b:b + 1], scale=modT[:, 1, b:b + 1])
                last.then_inc(ht_ready, 1)

            modulate(0)

            def item_a(kind, j, u):
                b, dr, par = unit(u)
                it = (kind, j, u)
                src = flat(bank(it))
                half, c = divmod(j, NCH)
                if kind not in ("BT", "O", "LG", "ST", "PT"):
                    act.wait_ge(pro_ready, NUMBER[it] + 1)
                if kind in ("X", "Z"):
                    if it in ORDER[2:NFIRST]:
                        wait_item(act, *ORDER[NUMBER[it] - 2])
                    nc.scalar.activation(th_of(it), src, ACT.Tanh).then_inc(tanh_ready, 1)
                elif kind == "B":
                    if u > 0:
                        act.wait_ge(c_stored, 16 * u)
                    nc.scalar.activation(xdbl[:, j * CH:(j + 1) * CH], src[0:XD, :], ACT.Copy).then_inc(item_act, 1)
                elif kind == "DT":
                    then_wait(nc.scalar.activation(sp_e[:, j, :], src, ACT.Abs, bias=dtb(dr, half)))
                    nc.scalar.activation(sp_e[:, j, :], sp_e[:, j, :], ACT.Exp, scale=-1.0).then_inc(e_ready, 1)
                elif kind == "DU":
                    nc.scalar.activation(duT[par][:, c * BPC:(c + 1) * BPC, half * P:(half + 1) * P],
                                         src.rearrange("p (n d) -> p n d", n=BPC), ACT.Copy).then_inc(item_act, 1)
                elif kind == "LT":
                    nc.scalar.activation(lnT[:, u, j * CH:(j + 1) * CH], src, ACT.Identity, bias=modT[:, 3, u:u + 1],
                                         scale=modT[:, 4, u:u + 1]).then_inc(item_act, 1)
                elif kind == "YT":
                    nc.scalar.activation(yg[:, half, c * CH:(c + 1) * CH], src, ACT.Copy).then_inc(item_act, 1)

            def logs(u):
                for j in range(NH * NCH):
                    act.wait_ge(r_ready, dt_count(j, u))
                    nc.scalar.activation(sp_e[:, j, :], sp_e[:, j, :], ACT.Ln, bias=1.0).then_inc(ln_ready, 1)

            def exp_tile(e):
                u, s, half = e // (DS * NH), e // NH % DS, e % NH
                _, dr, par = unit(u)
                if s == 0:
                    act.wait_ge(delta_ready, dt_count(NCH * half + NCH - 1, u))
                if e >= 3:
                    act.wait_ge(scan_done, NCH * (e - 2))
                nc.scalar.activation(dA[:, e % 3, :], delta[par][:, half, :], ACT.Exp,
                                     scale=Aneg[:, dr, half, s:s + 1]).then_inc(da_ready, 1)

            def scale_block(g, n):
                u, s = divmod(g, DS)
                _, _, par = unit(u)
                return nc.scalar.activation(dBuT[:, g % 2, n, :], duT[par][:, n, :], ACT.Copy,
                                            scale=bT[:, par, n, s:s + 1])

            def scale_blocks(g, ns):
                u = g // DS
                if g % DS == 0:
                    wait_item(act, "DU", 3, u)
                    wait_item(act, "BT", 0, u)
                if g >= 2:
                    act.wait_ge(dbu_ready, NCH * NH * (g - 1))
                for n in ns:
                    last = scale_block(g, n)
                if n == NBLK - dve_blocks(g) - 1:
                    last.then_inc(dbut_act, 1)

            def logits_exp(b):
                wait_item(act, "LG", 0, b)
                rs = slice(b * NBLK, (b + 1) * NBLK)
                nc.scalar.activation(lg[:, rs, :], lg[:, rs, :], ACT.Exp).then_inc(exp_ready, 1)

            for k, j in FIRST_ITEMS:
                if (k, j) == ("B", 0):
                    modulate(1)
                if (k, j) == ("DU", 0):
                    logs(0)
                    exp_tile(0)
                item_a(k, j, 0)
            scale_blocks(0, range(NBLK - dve_blocks(0)))
            for e in range(NT):
                g, half = divmod(e, NH)
                if e + 1 < NT:
                    exp_tile(e + 1)
                if g + 1 < NG:
                    na = NBLK - dve_blocks(g + 1)
                    scale_blocks(g + 1, range(na // 2) if half == 0 else range(na // 2, na))
                if e and ENDS[e - 1] is not None:
                    item_a(*ENDS[e - 1])
                if e % (DS * NH) == LN_AT and g // DS + 1 < NU:
                    logs(g // DS + 1)
                if e == NH * DS * (NU - 1) + SOFTMAX_AT - 1:
                    logits_exp(0)
            for k, j in LAST_ITEMS:
                item_a(k, j, NU - 1)

            def gathered_tokens(b):
                act.wait_ge(gathered, b + 1)
                nc.scalar.activation(exT[:, b, :], dBu[0][:, :], ACT.Identity,
                                     bias=modT[:, 3, b:b + 1], scale=modT[:, 4, b:b + 1]).then_inc(ext_ready, 1)

            def slots_softmax(b):
                act.wait_ge(slots_shifted, b + 1)
                nc.scalar.activation(slg[:, b], slg[:, b], ACT.Exp).then_inc(slots_exp, 1)

            def keep_turned(b, m):
                q, c = divmod(m, NCH)
                act.wait_ge(turned, b * 2 * NPAIR + m + 1)
                nc.scalar.activation(onehotT[:, b, q, c * BPC:(c + 1) * BPC, :], yT[:, 1, c * BPC:(c + 1) * BPC],
                                     ACT.Copy).then_inc(kept_act, 1)

            def keep_down(b, q):
                act.wait_ge(down_ready, b * NPAIR + q + 1)
                for e in (2 * q, 2 * q + 1):
                    last = nc.scalar.activation(eoT[:, e, :], down_bank(q)[:, e % 2 * TOPK:(e % 2 + 1) * TOPK], ACT.Identity,
                                                bias=b2g[:, b, e:e + 1], scale=modT[:, 5, b:b + 1])
                last.then_inc(eot_ready, 1)

            def hidden(b, q):
                act.wait_ge(up_ready, b * NPAIR + q + 1)
                if q >= 2:
                    act.wait_ge(down_ready, b * NPAIR + q - 1)
                for i in range(2):
                    for c in range(FC):
                        at = (i * FC + c) * TOPK
                        last = nc.scalar.activation(hid[:, q % 2, i, c, :], up_bank(q)[:, at:at + TOPK],
                                                    ACT.Gelu_apprx_tanh, bias=b1c[:, 2 * q + i, c:c + 1])
                last.then_inc(gelu_ready, 1)

            gathered_tokens(0)
            slots_softmax(0)
            def keep_eo(b, q):
                act.wait_ge(gcol_ready, 1)
                act.wait_ge(eo_turned, b * NPAIR + q + 1)
                nc.scalar.activation(eo[:, b, q, :], down_bank(q)[:, P:2 * P], ACT.Copy,
                                     scale=gcol[:, b, q:q + 1]).then_inc(eo_ready, 1)

            for q in range(NPAIR):
                hidden(0, q)
                if q == NPAIR - 2:
                    for k, j in NORM_ITEMS[0:2]:
                        item_a(k, j, 1)
                keep_turned(0, 2 * q)
                keep_turned(0, 2 * q + 1)
                if q == NPAIR - 2:
                    logits_exp(1)
                if q:
                    keep_down(0, q - 1)
                if q >= 2:
                    keep_eo(0, q - 2)
            keep_down(0, NPAIR - 1)
            keep_eo(0, NPAIR - 2)
            keep_eo(0, NPAIR - 1)
            gathered_tokens(1)
            slots_softmax(1)
            for q in range(NPAIR):
                hidden(1, q)
                keep_turned(1, 2 * q)

        @block.vector
        def _(dve):
            cnt = [0]

            def step(ins):
                cnt[0] += 1
                ins.then_inc(dve_step, 1)
                dve.wait_ge(dve_step, cnt[0])

            def x_stats(b):
                rows = range(b * NBLK, (b + 1) * NBLK)
                rs = slice(b * NBLK, (b + 1) * NBLK)
                dve.wait_ge(s_x, 16 * (b + 1))
                for n in rows:
                    last = nc.vector.bn_stats(st[:, n, :], x[:, b, n % NBLK, :])
                step(last)
                for n in rows:
                    last = nc.vector.bn_aggr(mv[:, n, :], st[:, n, :])
                step(last)
                nc.vector.tensor_scalar(rstd[:, rs], mv[:, rs, 1], EPS, None, ALU.add).then_inc(xvar_ready, 1)

            def x_norm(b):
                dve.wait_ge(xrstd_ready, b + 1)
                for n in range(NBLK):
                    r = b * NBLK + n
                    last = nc.vector.tensor_scalar(acc[:, b, n, :], x[:, b, n, :], mv[:, r, 0:1], rstd[:, r:r + 1],
                                                   ALU.subtract, ALU.mult)
                last.then_inc(xn_ready, 1)

            x_stats(0)
            dve.wait_ge(s_m, 16)
            dve.wait_ge(tanhc_ready, 1)
            step(nc.vector.tensor_scalar(scT[:, 1, :], cT, 0.5, None, ALU.mult))
            step(nc.vector.scalar_tensor_tensor(scT[:, 2, :], scT[:, 0, :], 1.0, scT[:, 1, :], ALU.add, ALU.mult))
            for b in range(NB):
                last = nc.vector.tensor_copy(scB[:, b, :], scT[:, 2, b:b + 1].to_broadcast([P, P]))
            last.then_inc(siluc_ready, 1)
            x_norm(0)
            dve.wait_ge(s_w, 32)
            step(nc.vector.tensor_scalar(biasc, biasc, 0.5, None, ALU.mult))
            step(nc.vector.tensor_copy(part16[:, 0, :], biasc))
            step(nc.vector.tensor_copy(part32[:, :, 0], part16[:, 0, :]))
            step(nc.vector.tensor_tensor(part32[:, :, 2], biasc, part32[:, :, 0], ALU.subtract))
            step(nc.vector.tensor_copy(part16[:, 1, :], part32[:, :, 2]))
            step(nc.vector.tensor_copy(part32[:, :, 1], part16[:, 1, :]))
            nc.vector.tensor_tensor(part32[:, :, 2], part32[:, :, 2], part32[:, :, 1],
                                    ALU.subtract).then_inc(parts_ready, 1)
            dve.wait_ge(mod_ready, 1)
            step(nc.vector.tensor_copy(modT[:, :, :], pro[:, 0:6 * NB].rearrange("p (j b) -> p j b", j=6)))
            nc.vector.tensor_scalar(modT[:, 1, :], modT[:, 1, :], 1.0, None, ALU.add)
            nc.vector.tensor_scalar(modT[:, 4, :], modT[:, 4, :], 1.0, None, ALU.add).then_inc(modt_ready, 1)
            for dr in range(2):
                for k in range(DC):
                    last = nc.vector.scalar_tensor_tensor(wtap[:, dr, k, :], convw[:, dr, k, :], 0.5, inx[:, dr, :],
                                                          ALU.mult, ALU.mult)
            last.then_inc(weights_ready, 1)
            dve.wait_ge(parts_turned, 1)
            nc.vector.tensor_copy(bias3[:, :, :, :].rearrange("p d h c -> p (d h c)"),
                                  dBu[1][0:3, :]).then_inc(bias_ready, 1)

            def other_weights():
                nc.vector.tensor_scalar(wz, wz, 0.5, None, ALU.mult)
                dve.wait_ge(aexp_ready, 1)
                nc.vector.tensor_scalar(Aneg[:, :, :, :], Aneg[:, :, :, :], -1.0, None, ALU.mult)
                dve.wait_ge(s_c, 10)
                for dr in range(2):
                    for half in range(NH):
                        at = WAT["dskip"] + dr * NH + half
                        last = nc.vector.tensor_scalar(dskip[:, dr, half, :], ident[:, :], wp[:, at:at + 1], None, ALU.mult)
                last.then_inc(weights_ready, 1)

            def clamp_gate(out, g, sign, size):
                step(nc.vector.tensor_scalar(sign, g, 0.0, 2.0, ALU.is_ge, ALU.mult))
                step(nc.vector.scalar_tensor_tensor(size, g, -1.0, g, ALU.mult, ALU.max))
                step(nc.vector.tensor_scalar(size, size, 0.25, None, ALU.max))
                step(nc.vector.scalar_tensor_tensor(out, sign, -1.0, size, ALU.add, ALU.mult))

            def gates():
                dve.wait_ge(gab_ready, 1)
                step(nc.vector.tensor_copy(gtemp[:, 0, :], dBu[0][:, 0:NB * D]))
                clamp_gate(gtemp[:, 0, :], gtemp[:, 0, :], gtemp[:, 1, :], gtemp[:, 2, :])
                dve.wait_ge(s_v, 32)
                for b in range(NB):
                    ga = gtemp[:, 0, b * D:(b + 1) * D]
                    nc.vector.tensor_tensor(g1[:, b, :], ga, lnw, ALU.mult)
                    step(nc.vector.tensor_tensor(g0[:, b, :], ga, lnb, ALU.mult))
                clamp_gate(modT[:, 5, :], modT[:, 5, :], scT[:, 0, :], scT[:, 1, :])
                for b in range(NB):
                    last = nc.vector.tensor_scalar(b2g[:, b, :], w("b2"), modT[:, 5, b:b + 1], None, ALU.mult)
                last.then_inc(gab_kept, 1)

            def add_ln_b():
                for b in range(NB):
                    step(nc.vector.tensor_tensor(x[:, b], x[:, b], g0[:, b:b + 1, :].to_broadcast([P, NBLK, D]), ALU.add))

            def item_v(kind, j, u):
                b, dr, par = unit(u)
                it = (kind, j, u)
                src = flat(bank(it))
                half, c = divmod(j, NCH)
                if kind == "X":
                    dve.wait_ge(tanh_ready, count_of(it, ("X", "Z")))
                    nc.vector.scalar_tensor_tensor(xc[par][:, half, c * CH:(c + 1) * CH], th_of(it), 1.0, src,
                                                   ALU.add, ALU.mult).then_inc(item_dve, 1)
                elif kind == "Z":
                    dve.wait_ge(tanh_ready, count_of(it, ("X", "Z")))
                    nc.vector.scalar_tensor_tensor(gz[par][:, 2 * j:2 * j + 2, :].rearrange("p n d -> p (n d)"),
                                                   th_of(it), 1.0, src, ALU.add, ALU.mult).then_inc(item_dve, 1)
                elif kind == "BT":
                    dve.wait_ge(pro_ready, NUMBER[it] + 1)
                    nc.vector.tensor_copy(bT[:, par, :, :],
                                          src[:, 0:NBLK * 2 * DS].rearrange("p (n s) -> p n s", n=NBLK)[:, :, 0:DS]
                                          ).then_inc(item_dve, 1)
                elif kind == "DT":
                    out = delta[par][:, half, c * CH:(c + 1) * CH]
                    dve.wait_ge(e_ready, dt_count(j, u))
                    nc.vector.tensor_scalar(sp_w[:, j, :], sp_e[:, j, :], 1.0, -1.0, ALU.add, ALU.add).then_inc(w_ready, 1)
                    nc.vector.tensor_scalar(out, src, dtb(dr, half), 0.0, ALU.add, ALU.max).then_inc(item_dve, 1)
                elif kind == "LG":
                    rs = slice(u * NBLK, (u + 1) * NBLK)
                    logits = src[:, 0:NBLK * E].rearrange("p (r e) -> p r e", e=E)
                    dve.wait_ge(pro_ready, NUMBER[it] + 1)
                    step(nc.vector.tensor_reduce(lmax[:, rs], logits, AX.X, ALU.max))
                    nc.vector.tensor_tensor(lg[:, rs, :], logits, lmax[:, rs].unsqueeze(2).to_broadcast([P, NBLK, E]),
                                            ALU.subtract).then_inc(item_dve, 1)
                elif kind == "ST":
                    dve.wait_ge(pro_ready, NUMBER[it] + 1)
                    nc.vector.tensor_copy(smT[:, j * CH:(j + 1) * CH], src[0:E, :]).then_inc(item_dve, 1)
                elif kind == "PT":
                    dve.wait_ge(pro_ready, NUMBER[it] + 1)
                    nc.vector.tensor_copy(posT[:, u].rearrange("p n e -> p (n e)"), src[:, 0:NBLK * E]).then_inc(item_dve, 1)
                elif kind == "O":
                    dst = acc[:, b, j * BPC:(j + 1) * BPC, :].rearrange("p n d -> p (n d)")
                    dve.wait_ge(pro_ready, NUMBER[it] + 1)
                    if dr == 0:
                        nc.vector.tensor_copy(dst, src).then_inc(item_dve, 1)
                    else:
                        nc.vector.tensor_tensor(dst, src, dst, ALU.add).then_inc(item_dve, 1)

            def norm_stage(b, stage):
                rows = range(b * NBLK, (b + 1) * NBLK)
                rs = slice(b * NBLK, (b + 1) * NBLK)
                src = acc if stage < 5 else x
                if stage == 0:
                    wait_item(dve, "O", 1, 2 * b + 1)
                if stage in (0, 5):
                    for n in rows:
                        last = nc.vector.bn_stats(st[:, n, :], src[:, b, n % NBLK, :])
                    step(last)
                elif stage in (1, 6):
                    for n in rows:
                        last = nc.vector.bn_aggr(mv[:, n, :], st[:, n, :])
                    step(last)
                    nc.vector.tensor_scalar(rstd[:, rs], mv[:, rs, 1], EPS, None, ALU.add).then_inc(var_ready, 1)
                elif stage in (2, 7):
                    dve.wait_ge(rstd_ready, 2 * b + (1 if stage == 2 else 2))
                    dst = acc if stage == 2 else lnx
                    for r in rows:
                        last = nc.vector.tensor_scalar(dst[:, b, r % NBLK, :], src[:, b, r % NBLK, :], mv[:, r, 0:1],
                                                       rstd[:, r:r + 1], ALU.subtract, ALU.mult)
                    if stage == 2:
                        step(last)
                    else:
                        last.then_inc(lnx_ready, 1)
                elif stage == 3:
                    step(nc.vector.tensor_tensor(acc[:, b], acc[:, b], g1[:, b:b + 1, :].to_broadcast([P, NBLK, D]),
                                                 ALU.mult))
                elif stage == 4:
                    step(nc.vector.tensor_tensor(x[:, b], x[:, b], acc[:, b], ALU.add))

            def finish_delta(j, u):
                _, _, par = unit(u)
                half, c = divmod(j, NCH)
                out = delta[par][:, half, c * CH:(c + 1) * CH]
                wait_item(dve, "DT", j, u)
                dve.wait_ge(ln_ready, dt_count(j, u))
                step(nc.vector.tensor_tensor(sp_e[:, j, :], sp_e[:, j, :], sp_w[:, j, :], ALU.add))
                nc.vector.tensor_tensor(out, out, sp_e[:, j, :], ALU.add).then_inc(delta_ready, 1)

            def scale_blocks(g):
                u, s = divmod(g, DS)
                _, _, par = unit(u)
                if s == 0:
                    wait_item(dve, "DU", 3, u)
                    wait_item(dve, "BT", 0, u)
                if g >= 2:
                    dve.wait_ge(dbu_ready, NCH * NH * (g - 1))
                for n in range(NBLK - dve_blocks(g), NBLK):
                    last = nc.vector.tensor_scalar(dBuT[:, g % 2, n, :], duT[par][:, n, :],
                                                   bT[:, par, n, s:s + 1], None, ALU.mult)
                last.then_inc(dbut_dve, 1)

            def scan_chunk(e, i):
                u, q = e // (DS * NH), NCH * e + i
                c = chunks(u)[i]
                if i == 0:
                    dve.wait_ge(da_ready, e + 1)
                    if e >= 3:
                        dve.wait_ge(hc_done, e - 2)
                dve.wait_ge(dbu_ready, q + 1)
                if i:
                    dve.wait_ge(scan_done, q)
                lo, hi = c * CH, (c + 1) * CH
                if u % 2 == 0:
                    init = hs[:, e % 3, lo - 1:lo] if i else 0.0
                    nc.vector.tensor_tensor_scan(hs[:, e % 3, lo:hi], dA[:, e % 3, lo:hi], dBu[q % 3][:, :],
                                                 init, ALU.mult, ALU.add).then_inc(scan_done, 1)
                else:
                    init = hs[:, e % 3, hi:hi + 1] if i else 0.0
                    nc.vector.tensor_tensor_scan(hs[:, e % 3, lo:hi][:, ::-1], dA[:, e % 3, lo:hi][:, ::-1],
                                                 dBu[q % 3][:, ::-1], init, ALU.mult, ALU.add).then_inc(scan_done, 1)

            def gate(u, half):
                _, _, par = unit(u)
                dve.wait_ge(yacc_done, NH * DS * (u + 1) - (NH - 1 - half))
                wait_item(dve, "Z", 3, u)
                at = gz[par][:, :, half * P:(half + 1) * P]
                nc.vector.tensor_tensor(at, yT[:, half], at, ALU.mult).then_inc(gate_done, 1)

            def softmax(b):
                rs = slice(b * NBLK, (b + 1) * NBLK)
                dve.wait_ge(exp_ready, b + 1)
                step(nc.vector.tensor_reduce(lsum[:, rs], lg[:, rs, :], AX.X, ALU.add))
                step(nc.vector.reciprocal(lsum[:, rs], lsum[:, rs]))
                nc.vector.tensor_tensor(sm[:, b], lg[:, rs, :], lsum[:, rs].unsqueeze(2).to_broadcast([P, NBLK, E]),
                                        ALU.mult).then_inc(sm_ready, 1)

            def choose(b, k):
                r, marking = divmod(k, 2)
                src = smT if r == 0 else smW[b]
                if k == 0:
                    wait_item(dve, "ST", 1, b)
                if not marking:
                    step(nc.vector.max(top8[:, r, :], src))
                else:
                    step(nc.vector.match_replace(smW[b], top8[:, r, :], src, -1.0))

            def slots(b, stage):
                if stage == 0:
                    step(nc.vector.tensor_scalar(smT, smW[b], 0.0, None, ALU.is_lt))
                elif stage == 1:
                    dve.wait_ge(ones_ready, b + 1)
                    step(nc.vector.tensor_tensor_scan(smW[b], onesr[b], smT, 0.0, ALU.mult, ALU.add))
                else:
                    nc.vector.tensor_tensor(smW[b], smW[b], smT, ALU.mult).then_inc(pos_ready, 1)

            def build_onehot(b, ns):
                wait_item(dve, "PT", 0, b)
                for n in ns:
                    nc.vector.tensor_tensor(onehot[:, b, n, :].rearrange("p (e k) -> p e k", e=E),
                                            posT[:, b, n, :].unsqueeze(2).to_broadcast([P, E, TOPK]),
                                            iotak[:, :].unsqueeze(1).to_broadcast([P, E, TOPK]),
                                            ALU.is_equal).then_inc(onehot_ready, 1)

            def slots_shift(b):
                slogits = dBu[0][:, 0:NPAIR * E].rearrange("p (q e) -> p q e", e=E)
                dve.wait_ge(slogits_ready, b + 1)
                step(nc.vector.tensor_reduce(smax[:, b], slogits, AX.X, ALU.max))
                nc.vector.tensor_tensor(slg[:, b], slogits, smax[:, b].unsqueeze(2).to_broadcast([P, NPAIR, E]),
                                        ALU.subtract).then_inc(slots_shifted, 1)

            def slots_weights(b):
                dve.wait_ge(slots_exp, b + 1)
                step(nc.vector.tensor_reduce(smax[:, b], slg[:, b], AX.X, ALU.add))
                step(nc.vector.reciprocal(smax[:, b], smax[:, b]))
                step(nc.vector.tensor_tensor(gtmp[:, b], slg[:, b], emask[:, :, :], ALU.mult))
                step(nc.vector.tensor_reduce(gcol[:, b], gtmp[:, b], AX.X, ALU.add))
                ins = nc.vector.tensor_tensor(gcol[:, b], gcol[:, b], smax[:, b], ALU.mult)
                if b == 0:
                    ins.then_inc(gcol_ready, 1)
                else:
                    step(ins)

            def add_experts(b):
                for c in range(NCH):
                    dve.wait_ge(scattered, NCH * b + c + 1)
                    ns = slice(c * BPC, (c + 1) * BPC)
                    nc.vector.tensor_tensor(x[:, b, ns, :], yT[:, 0, ns, :], x[:, b, ns, :], ALU.add).then_inc(x2_ready, 1)

            for k, j in FIRST_ITEMS:
                if (k, j) == ("DU", 0):
                    for i in range(4):
                        finish_delta(i, 0)
                    add_ln_b()
                item_v(k, j, 0)
                if (k, j) == ("X", 0):
                    x_stats(1)
                elif (k, j) == ("X", 2):
                    x_norm(1)
                elif (k, j) == ("X", 1):
                    gates()
                elif (k, j) == ("X", 3):
                    other_weights()
            scale_blocks(0)
            for e in range(NT):
                g, half = divmod(e, NH)
                u, s = divmod(g, DS)
                scan_chunk(e, 0)
                if u > 0 and e % (NH * DS) in (1, 2):
                    gate(u - 1, e % (NH * DS) - 1)
                for j in finish_at(e):
                    finish_delta(j, u + 1)
                if e and ENDS[e - 1] is not None:
                    item_v(*ENDS[e - 1])
                scan_chunk(e, 1)
                if half == 0 and g + 1 < NG:
                    scale_blocks(g + 1)
                if e - NH * DS * (NU - 2) in NORM_AT:
                    norm_stage(0, NORM_AT[e - NH * DS * (NU - 2)])
                if u == NU - 1:
                    t = e % (NH * DS)
                    if t == SOFTMAX_AT:
                        softmax(0)
                    elif t in CHOOSE_STEPS:
                        choose(0, CHOOSE_STEPS.index(t))
                    elif SLOTS_AT <= t < SLOTS_AT + 3:
                        slots(0, t - SLOTS_AT)
            item_v("PT", 0, 0)
            build_onehot(0, range(0, 6))
            gate(NU - 1, 0)
            gate(NU - 1, 1)
            build_onehot(0, range(6, NBLK))
            for k, j in LAST_ITEMS:
                item_v(k, j, NU - 1)

            for stage in range(8):
                if stage == 2:
                    slots_shift(0)
                if stage == 7:
                    slots_weights(0)
                norm_stage(1, stage)
            item_v("LG", 0, 1)
            softmax(1)
            for j in range(NCH):
                item_v("ST", j, 1)
            for k in range(2 * (TOPK // 8)):
                choose(1, k)
            for stage in range(3):
                slots(1, stage)
            item_v("PT", 0, 1)
            build_onehot(1, range(NBLK))
            add_experts(0)
            slots_shift(1)
            slots_weights(1)

            def keep_down(b, q):
                dve.wait_ge(down_ready, b * NPAIR + q + 1)
                for e in (2 * q, 2 * q + 1):
                    last = nc.vector.tensor_scalar(eoT[:, e, :], down_bank(q)[:, e % 2 * TOPK:(e % 2 + 1) * TOPK], modT[:, 5, b:b + 1],
                                                   b2g[:, b, e:e + 1], ALU.mult, ALU.add)
                last.then_inc(eot_ready, 1)

            def keep_eo(b, q):
                dve.wait_ge(eo_turned, b * NPAIR + q + 1)
                nc.vector.tensor_scalar(eo[:, b, q, :], down_bank(q)[:, P:2 * P], gcol[:, b, q:q + 1], None,
                                        ALU.mult).then_inc(eo_ready, 1)

            for q in range(NPAIR):
                dve.wait_ge(turned, 2 * NPAIR + 2 * q + 2)
                nc.vector.tensor_copy(onehotT[:, 1, q, BPC:NBLK, :], yT[:, 1, BPC:NBLK]).then_inc(kept_dve, 1)
                if q:
                    keep_down(1, q - 1)
                if q >= 2:
                    keep_eo(1, q - 2)
            keep_down(1, NPAIR - 1)
            keep_eo(1, NPAIR - 2)
            keep_eo(1, NPAIR - 1)
            add_experts(1)

        @block.tensor
        def _(pe):
            def mm(out, lhsT, rhs, start, stop):
                return nc.tensor.matmul(out, lhsT, rhs, start=start, stop=stop, skip_group_check=True)

            def turn(out, in_, start, idn=None):
                return nc.tensor.matmul(out, in_, ident[:, :] if idn is None else idn, start=start, stop=True,
                                        is_transpose=True, skip_group_check=True)

            pe.wait_ge(s_c, 10)
            pe.wait_ge(siluc_ready, 1)
            for j in range(6):
                last = mm(pro[:, NB * j:NB * (j + 1)], wmod[:, j * D:(j + 1) * D], scT[:, 2, :], True, True)
            last.then_inc(mod_ready, 1)

            def turn_xn(b):
                pe.wait_ge(xn_ready, b + 1)
                for n in range(NBLK):
                    dst = yT[:, 0, n, :] if b == 0 else dBu[1 + n // BPC][:, n % BPC * P:(n % BPC + 1) * P]
                    last = turn(dst, acc[:, b, n, :], True)
                last.then_inc(xn_turned, 1)

            turn_xn(0)
            pe.wait_ge(parts_ready, 1)
            for k in range(NBIAS):
                last = turn(dBu[1][0:3, k * P:(k + 1) * P], part32[:, k, :], True)
            last.then_inc(parts_turned, 1)
            for b in range(NB):
                last = mm(dBu[0][:, b * D:(b + 1) * D], scB[:, b, :], wmod[:, 2 * D:3 * D], True, True)
            last.then_inc(gab_ready, 1)
            pe.wait_ge(ht_ready, 1)
            pe.wait_ge(bias_ready, 1)
            pe.wait_ge(weights_ready, 1)
            pe.wait_ge(modt_ready, 1)

            def item_t(it, part):
                kind, j, u = it
                b, dr, par = unit(u)
                n_it = NUMBER[it]
                dst = flat(bank(it))
                half, c = divmod(j, NCH)
                if part == 0 and n_it >= 5:
                    wait_item(pe, *ORDER[n_it - (5 if n_it < NFIRST else 1 if n_it < NLAST + 1 else 2)])
                    if n_it == NFIRST:
                        for k in range(2, 6):
                            wait_item(pe, *ORDER[n_it - k])
                if kind == "X":
                    at = c * CH + (part if dr == 0 else 2 * PAD - part)
                    last = mm(dst, wtap[:, dr, part, half * P:(half + 1) * P], hT[:, b, at:at + CH], part == 0, False)
                    if part == DC - 1:
                        last = mm(dst, bias3[:, dr, half, :], ones3[:, 0:1].to_broadcast([3, CH]), False, True)
                elif kind == "Z":
                    at = PAD + (2 * j + part) * P
                    last = mm(dst[:, part * DI:(part + 1) * DI], hT[:, b, at:at + P], wz[:, dr, :], True, True)
                elif kind == "B":
                    if part == 0:
                        for h in range(NH):
                            wait_item(pe, "X", h * NCH + j, u)
                    last = mm(dst[0:XD, :], xproj[:, dr, part, :], xc[par][:, part, j * CH:(j + 1) * CH],
                              part == 0, part == NH - 1)
                elif kind == "BT":
                    if part == 0:
                        wait_item(pe, "B", 1, u)
                    for n in range(part * BPC, (part + 1) * BPC):
                        last = turn(dst[:, n * 2 * DS:(n + 1) * 2 * DS], xdbl[DR:XD, n * P:(n + 1) * P], True,
                                    ident[DR:XD, DR:XD])
                elif kind == "DT":
                    at = c * CH + part * CH // 2
                    last = mm(dst[:, part * CH // 2:(part + 1) * CH // 2], dtw[:, dr, half * P:(half + 1) * P],
                              xdbl[0:DR, at:at + CH // 2], True, True)
                elif kind == "DU":
                    if part == 0:
                        pe.wait_ge(du_ready, dt_count(j, u))
                    for i in (2 * part, 2 * part + 1):
                        last = turn(dst[:, i * P:(i + 1) * P], sp_w[:, j, i * P:(i + 1) * P], True)
                elif kind == "YT":
                    if part == 0:
                        pe.wait_ge(gate_done, NH * (u + 1))
                    for i in (2 * part, 2 * part + 1):
                        last = turn(dst[:, i * P:(i + 1) * P], gz[par][:, c * BPC + i, half * P:(half + 1) * P], True)
                elif kind == "LT":
                    if part == 0:
                        pe.wait_ge(lnx_ready, u + 1)
                    for i in (2 * part, 2 * part + 1):
                        last = turn(dst[:, i * P:(i + 1) * P], lnx[:, u, j * BPC + i, :], True)
                elif kind == "LG":
                    if part == 0:
                        wait_item(pe, "LT", 1, u)
                    for n in range(part * BPC, (part + 1) * BPC):
                        last = mm(dst[:, n * E:(n + 1) * E], lnT[:, u, n * P:(n + 1) * P], w("wg"), True, True)
                elif kind == "ST":
                    if part == 0:
                        pe.wait_ge(sm_ready, u + 1)
                    for i in (2 * part, 2 * part + 1):
                        last = turn(dst[0:E, i * P:(i + 1) * P], sm[:, u, j * BPC + i, :], True)
                elif kind == "PT":
                    if part == 0:
                        pe.wait_ge(pos_ready, u + 1)
                    for n in range(part * BPC, (part + 1) * BPC):
                        last = turn(dst[:, n * E:(n + 1) * E], smW[u][:, n * P:(n + 1) * P], True, ident[0:E, 0:E])
                elif kind == "O":
                    if part == 0:
                        wait_item(pe, "YT", 3, u)
                    for i in (2 * part, 2 * part + 1):
                        n = j * BPC + i
                        o = dst[:, i * D:(i + 1) * D]
                        if dr == 0:
                            turn(o, hT[:, b, PAD + n * P:PAD + (n + 1) * P], True)
                        for h in range(NH):
                            last = mm(o, yg[:, h, n * P:(n + 1) * P], outproj[:, dr, h, :],
                                      dr == 1 and h == 0, h == NH - 1)
                if part == parts_of(kind) - 1:
                    last.then_inc(pro_ready, 1)

            def dbu_chunk(e, i):
                u, half = e // (DS * NH), e % NH
                g, q = e // NH, NCH * e + i
                c = chunks(u)[i]
                if half == 0 and i == 0:
                    pe.wait_ge(dbut_act, g + 1)
                    pe.wait_ge(dbut_dve, g + 1)
                if q >= 3:
                    pe.wait_ge(scan_done, q - 2)
                for k in range(BPC):
                    last = turn(dBu[q % 3][:, k * P:(k + 1) * P],
                                dBuT[:, g % 2, c * BPC + k, half * P:(half + 1) * P], True)
                last.then_inc(dbu_ready, 1)

            def y_start(u, half):
                _, dr, par = unit(u)
                if u > 0:
                    pe.wait_ge(gate_done, NH * (u - 1) + half + 1)
                for n in range(NBLK):
                    mm(yT[:, half, n, :], xc[par][:, half, n * P:(n + 1) * P], dskip[:, dr, half, :],
                       n % BPC == 0, True)

            def y_add(e):
                half = e % NH
                pe.wait_ge(hc_done, e + 1)
                for n in range(NBLK):
                    last = turn(yT[:, half, n, :], hc[:, e % 3, n * P:(n + 1) * P], False)
                last.then_inc(yacc_done, 1)

            for k, j in FIRST_ITEMS:
                if (k, j) == ("B", 0):
                    turn_xn(1)
                    pe.wait_ge(weights_ready, 2)
                    pe.wait_ge(s_v, 32)
                if (k, j) == ("DU", 0):
                    pe.wait_ge(gab_kept, 1)
                    pe.wait_ge(ht_ready, 2)
                for part in range(parts_of(k)):
                    item_t((k, j, 0), part)
            for i in range(NCH):
                dbu_chunk(0, i)
            for e in range(NT):
                u, t = divmod(e, DS * NH)
                for i in range(NCH):
                    if e + 1 < NT:
                        dbu_chunk(e + 1, i)
                for p in PARTS[e]:
                    item_t(*p)
                if t in (2, 3):
                    y_start(u, t - 2)
                if e >= 2:
                    y_add(e - 2)
            def gather(b, ns):
                for n in ns:
                    pe.wait_ge(onehot_ready, b * NBLK + n + 1)
                    last = mm(dBu[0][:, :], lnx[:, b, n, :], onehot[:, b, n, :], n == 0, n == NBLK - 1)
                if n == NBLK - 1:
                    last.then_inc(gathered, 1)

            def slot_logits(b):
                pe.wait_ge(ext_ready, b + 1)
                for q in range(NPAIR):
                    last = mm(dBu[0][:, q * E:(q + 1) * E], exT[:, b, q * P:(q + 1) * P], w("wg"), True, True)
                last.then_inc(slogits_ready, 1)

            def up(b, q):
                if q >= 2:
                    pe.wait_ge(gelu_ready, b * NPAIR + q - 1)
                for i in range(2):
                    for c in range(FC):
                        at = (i * FC + c) * TOPK
                        e = 2 * q + i
                        last = mm(up_bank(q)[:, at:at + TOPK], w1s[:, e, c * P:(c + 1) * P],
                                  exT[:, b, e * TOPK:(e + 1) * TOPK], True, True)
                last.then_inc(up_ready, 1)

            def down(b, q):
                pe.wait_ge(gelu_ready, b * NPAIR + q + 1)
                if q == 0:
                    pe.wait_ge(slots_shifted, b + 1)
                if q >= 2:
                    pe.wait_ge(eo_ready, b * NPAIR + q - 1)
                for i in range(2):
                    e = 2 * q + i
                    for c in range(FC):
                        last = mm(down_bank(q)[:, e % 2 * TOPK:(e % 2 + 1) * TOPK], w2s[e][:, c, :], hid[:, q % 2, i, c, :],
                                  c == 0, c == FC - 1)
                last.then_inc(down_ready, 1)

            def turn_onehot(b, m):
                q, c = divmod(m, NCH)
                if b == 0 and m >= 2:
                    pe.wait_ge(kept_act, m - 1)
                elif b == 1 and m < 2:
                    pe.wait_ge(kept_act, 2 * NPAIR)
                elif b == 1:
                    pe.wait_ge(kept_dve if c else kept_act, (0 if c else 2 * NPAIR) + m // 2)
                for n in range(c * BPC, (c + 1) * BPC):
                    last = turn(yT[:, 1, n, :], onehot[:, b, n, q * P:(q + 1) * P], True)
                last.then_inc(turned, 1)

            def turn_eo(b, q):
                pe.wait_ge(eot_ready, b * NPAIR + q + 1)
                last = turn(down_bank(q)[:, P:2 * P], eoT[:, 2 * q:2 * q + 2, :].rearrange("p e k -> p (e k)"), True)
                last.then_inc(eo_turned, 1)

            def experts(b):
                if b == 0:
                    pe.wait_ge(s_w1, 16)
                    pe.wait_ge(s_w2, 48)
                else:
                    pe.wait_ge(x2_ready, 2)
                for q in range(NPAIR):
                    up(b, q)
                    turn_onehot(b, 2 * q)
                    if b == 0 and q == NPAIR - 2:
                        norm_items(NORM_ITEMS[0:2])
                    turn_onehot(b, 2 * q + 1)
                    if b == 0 and q == NPAIR - 2:
                        norm_items(NORM_ITEMS[2:3])
                    if q:
                        down(b, q - 1)
                    if q >= 2:
                        turn_eo(b, q - 2)
                    if b == 0 and q == NPAIR - 2:
                        norm_items(NORM_ITEMS[3:5])

            def norm_items(items):
                for k, j in items:
                    for part in range(parts_of(k)):
                        item_t((k, j, 1), part)

            def scatter(b, q):
                if q == 0:
                    pe.wait_ge(gelu_ready, (b + 1) * NPAIR)
                    if b == 0:
                        pe.wait_ge(kept_act, 2 * NPAIR)
                    else:
                        pe.wait_ge(kept_act, 3 * NPAIR)
                        pe.wait_ge(kept_dve, NPAIR)
                pe.wait_ge(eo_ready, b * NPAIR + q + 1)
                for n in range(NBLK):
                    last = mm(yT[:, 0, n, :], onehotT[:, b, q, n, :], eo[:, b, q, :], q == 0 and n % BPC == 0,
                              q == NPAIR - 1)
                    if q == NPAIR - 1 and n % BPC == BPC - 1:
                        last.then_inc(scattered, 1)

            y_add(NT - 2)
            pe.wait_ge(scan_done, NCH * NT)
            gather(0, range(0, 3))
            y_add(NT - 1)
            gather(0, range(3, 4))
            for k, j in LAST_ITEMS:
                for part in range(parts_of(k)):
                    item_t((k, j, NU - 1), part)

            gather(0, range(4, NBLK))
            slot_logits(0)
            experts(0)
            down(0, NPAIR - 1)
            turn_eo(0, NPAIR - 2)
            turn_eo(0, NPAIR - 1)
            for q in range(NPAIR):
                scatter(0, q)
            norm_items(NORM_ITEMS[5:])
            gather(1, range(NBLK))
            slot_logits(1)
            experts(1)
            down(1, NPAIR - 1)
            scatter(1, 0)
            turn_eo(1, NPAIR - 2)
            scatter(1, 1)
            turn_eo(1, NPAIR - 1)
            scatter(1, 2)
            scatter(1, 3)


def kernel(**inputs):
    import concourse.bacc as bacc
    from concourse.bass_utils import run_bass_kernel_spmd

    a = {k: np.asarray(v) for k, v in inputs.items()}

    def both(name, lay):
        return [lay(a[f"L0_attn_{name}_{d}"]) for d in "fb"]

    def halves(m):
        return m.reshape(NH, P, -1).transpose(1, 0, 2).reshape(P, -1)

    wpack = np.concatenate(
        both("A_log", halves) + both("D", halves)
        + both("in_proj", lambda m: m[:DI].T) + both("in_proj", lambda m: m[DI:].T)
        + both("x_proj", lambda m: halves(m.T)) + both("out_proj", lambda m: halves(m.T))
        + [a["L0_ffn_Wg"].T, a["L0_ffn_b1"].reshape(E, FC, P).transpose(2, 0, 1).reshape(P, -1), a["L0_ffn_b2"].T]
        + both("conv_b", halves) + both("dt_b", halves), axis=1)
    bcast = np.concatenate(both("conv_w", lambda m: m.T.reshape(-1)) + [a["L0_attn_ln_w"], a["L0_attn_ln_b"]])
    dtw = np.stack(both("dt_w", lambda m: m.T), axis=1)
    arrays = {"x_in": a["L0_attn_x"], "mod_in": np.concatenate([a["L0_c"].T, a["L0_wmod"]], axis=1),
              "wpack_in": wpack, "bcast_in": bcast, "dtw_in": dtw,
              "w1_in": a["L0_ffn_W1"], "w2_in": a["L0_ffn_W2"]}
    arrays = {k: np.ascontiguousarray(v) for k, v in arrays.items()}

    nc = bacc.Bacc("TRN2", target_bir_lowering=False, num_devices=1)
    aps = [nc.dram_tensor(k, v.shape, mybir.dt.from_np(v.dtype), kind="ExternalInput").ap() for k, v in arrays.items()]
    crow = nc.dram_tensor("c_rows", (NU, DS, L), mybir.dt.float32, kind="Internal").ap()
    out = nc.dram_tensor("out", (NB, L, D), mybir.dt.float32, kind="ExternalOutput").ap()
    build_block(nc, *aps, crow, out)
    r = run_bass_kernel_spmd(nc, [arrays], core_ids=[0])
    return r.results[0]["out"]
```
